# Optimizing a Trainium2 kernel written in Bass

```python
import numpy as np
import jax
import jax.numpy as jnp

def _softmax(x, axis=-1):
    return jax.nn.softmax(x, axis=axis)

def _gelu(x):
    return jax.nn.gelu(x, approximate=True)

def _silu(x):
    return jax.nn.silu(x)

def _sigmoid(x):
    return jax.nn.sigmoid(x)

def _layernorm(x, axis=-1, eps=1e-05):
    m = jnp.mean(x, axis=axis, keepdims=True)
    v = jnp.var(x, axis=axis, keepdims=True)
    return (x - m) / jnp.sqrt(v + eps)

def _scatter_add(tgt, idx, src, axis=0):
    return tgt.at[idx].add(src)

def _segment_sum(src, seg, n):
    return jax.ops.segment_sum(src, seg, n)
kernel_name = 'mk_recurrent_d1_jaxref_r4_78e0d2'

def setup_inputs(seed: int=0):
    np.random.seed(seed)
    _w = jnp.asarray

    def _L0_attn_setup():
        import jax, jax.numpy as jnp
        import numpy as np
        EMBED = 512
        HEADS = 16
        HEAD_DIM = EMBED // HEADS
        CHUNK = 128
        BASE = 10000.0
        EPS = 1e-06

        def _alibi_log_decay(h):
            slopes = 2.0 ** (-8.0 * (jnp.arange(h, dtype=jnp.float32) + 1.0) / h)
            return -slopes

        def _lrpe_rotate(x):
            b, n, h, d = x.shape
            half = d // 2
            theta = BASE ** (-2.0 * jnp.arange(half, dtype=jnp.float32) / d)
            ang = jnp.arange(n, dtype=jnp.float32)[:, None] * theta[None, :]
            cos = jnp.cos(ang)[None, :, None, :]
            sin = jnp.sin(ang)[None, :, None, :]
            x1, x2 = (x[..., :half], x[..., half:])
            return jnp.concatenate([x1 * cos - x2 * sin, x1 * sin + x2 * cos], axis=-1)

        def _lightning_attn(q, k, v, log_lam):
            b, n, h, d = q.shape
            C = CHUNK
            nc = n // C
            qc = q.reshape(b, nc, C, h, d).transpose(1, 0, 2, 3, 4)
            kc = k.reshape(b, nc, C, h, d).transpose(1, 0, 2, 3, 4)
            vc = v.reshape(b, nc, C, h, d).transpose(1, 0, 2, 3, 4)
            i = jnp.arange(C, dtype=jnp.float32)
            diff = i[:, None] - i[None, :]
            D = jnp.where(diff[None] >= 0, jnp.exp(log_lam[:, None, None] * diff[None]), 0.0)
            decay_q = jnp.exp(log_lam[None, :] * (i[:, None] + 1.0))
            decay_k = jnp.exp(log_lam[None, :] * (C - 1.0 - i[:, None]))
            lam_C = jnp.exp(log_lam * C)

            def step(S, qkv):
                qi, ki, vi = qkv
                scores = jnp.einsum('bthd,bshd->bhts', qi, ki) * D[None]
                o_intra = jnp.einsum('bhts,bshd->bthd', scores, vi)
                o_inter = jnp.einsum('bthd,bhde->bthe', qi * decay_q[None, :, :, None], S)
                S_new = lam_C[None, :, None, None] * S + jnp.einsum('bshd,bshe->bhde', ki * decay_k[None, :, :, None], vi)
                return (S_new, o_intra + o_inter)
            S0 = jnp.zeros((b, h, d, d), q.dtype)
            _, o = jax.lax.scan(step, S0, (qc, kc, vc))
            return o.transpose(1, 0, 2, 3, 4).reshape(b, n, h, d)

        def _gated_group_rmsnorm(o, gate, weight):
            b, n, d = o.shape
            x = o * jax.nn.sigmoid(gate)
            xg = x.reshape(b, n, HEADS, HEAD_DIM)
            ms = jnp.mean(xg * xg, axis=-1, keepdims=True)
            xg = xg * jax.lax.rsqrt(ms + EPS)
            return xg.reshape(b, n, d) * weight
        key = jax.random.key(seed)
        ks = jax.random.split(key, 8)
        b, n, d = (2, 512, EMBED)
        std = 0.02
        return {'x': jax.random.normal(ks[0], (b, n, d), jnp.float32), 'Wq': jax.random.normal(ks[1], (d, d), jnp.float32) * std, 'Wk': jax.random.normal(ks[2], (d, d), jnp.float32) * std, 'Wv': jax.random.normal(ks[3], (d, d), jnp.float32) * std, 'Wo': jax.random.normal(ks[4], (d, d), jnp.float32) * std, 'Wg1': jax.random.normal(ks[5], (d, HEAD_DIM), jnp.float32) * std, 'Wg2': jax.random.normal(ks[6], (HEAD_DIM, d), jnp.float32) * std, 'norm_weight': jnp.ones((d,), jnp.float32)}
    _L0_attn_in = _L0_attn_setup()

    def _L0_ffn_setup():
        import jax, jax.numpy as jnp
        import numpy as np
        B, S, D = (1, 512, 512)
        F = 128
        E = 16
        K = 4

        def _swiglu(x, wg, wu, wd):
            return jax.nn.silu(x @ wg) * (x @ wu) @ wd
        key = jax.random.key(seed)
        ks = jax.random.split(key, 10)
        s = 0.02
        return {'hidden_states': jax.random.normal(ks[0], (B, S, D), dtype=jnp.float32), 'gate_w': jax.random.normal(ks[1], (E, D), dtype=jnp.float32) * s, 'Wg': jax.random.normal(ks[2], (E, D, F), dtype=jnp.float32) * s, 'Wu': jax.random.normal(ks[3], (E, D, F), dtype=jnp.float32) * s, 'Wd': jax.random.normal(ks[4], (E, F, D), dtype=jnp.float32) * s, 'sWg': jax.random.normal(ks[5], (D, F), dtype=jnp.float32) * s, 'sWu': jax.random.normal(ks[6], (D, F), dtype=jnp.float32) * s, 'sWd': jax.random.normal(ks[7], (F, D), dtype=jnp.float32) * s, 'shared_gate_w': jax.random.normal(ks[8], (D, 1), dtype=jnp.float32) * s}
    _L0_ffn_in = _L0_ffn_setup()
    _d = {'L0_attn_x': _L0_attn_in['x'], 'L0_attn_Wq': _L0_attn_in['Wq'], 'L0_attn_Wk': _L0_attn_in['Wk'], 'L0_attn_Wv': _L0_attn_in['Wv'], 'L0_attn_Wo': _L0_attn_in['Wo'], 'L0_attn_Wg1': _L0_attn_in['Wg1'], 'L0_attn_Wg2': _L0_attn_in['Wg2'], 'L0_attn_norm_weight': _L0_attn_in['norm_weight'], 'L0_ffn_gate_w': _L0_ffn_in['gate_w'], 'L0_ffn_Wg': _L0_ffn_in['Wg'], 'L0_ffn_Wu': _L0_ffn_in['Wu'], 'L0_ffn_Wd': _L0_ffn_in['Wd'], 'L0_ffn_sWg': _L0_ffn_in['sWg'], 'L0_ffn_sWu': _L0_ffn_in['sWu'], 'L0_ffn_sWd': _L0_ffn_in['sWd'], 'L0_ffn_shared_gate_w': _L0_ffn_in['shared_gate_w']}
    _x0 = _d['L0_attn_x']
    _d['L0_attn_x'] = jax.random.normal(jax.random.fold_in(jax.random.key(seed), 1), (8, 512, 512), dtype=_x0.dtype)
    del _x0
    return _d

def reference(L0_attn_x, L0_attn_Wq, L0_attn_Wk, L0_attn_Wv, L0_attn_Wo, L0_attn_Wg1, L0_attn_Wg2, L0_attn_norm_weight, L0_ffn_gate_w, L0_ffn_Wg, L0_ffn_Wu, L0_ffn_Wd, L0_ffn_sWg, L0_ffn_sWu, L0_ffn_sWd, L0_ffn_shared_gate_w):

    def _L0_attn_ref(x, Wq, Wk, Wv, Wo, Wg1, Wg2, norm_weight):
        import jax, jax.numpy as jnp
        import numpy as np
        EMBED = 512
        HEADS = 16
        HEAD_DIM = EMBED // HEADS
        CHUNK = 128
        BASE = 10000.0
        EPS = 1e-06

        def _alibi_log_decay(h):
            slopes = 2.0 ** (-8.0 * (jnp.arange(h, dtype=jnp.float32) + 1.0) / h)
            return -slopes

        def _lrpe_rotate(x):
            b, n, h, d = x.shape
            half = d // 2
            theta = BASE ** (-2.0 * jnp.arange(half, dtype=jnp.float32) / d)
            ang = jnp.arange(n, dtype=jnp.float32)[:, None] * theta[None, :]
            cos = jnp.cos(ang)[None, :, None, :]
            sin = jnp.sin(ang)[None, :, None, :]
            x1, x2 = (x[..., :half], x[..., half:])
            return jnp.concatenate([x1 * cos - x2 * sin, x1 * sin + x2 * cos], axis=-1)

        def _lightning_attn(q, k, v, log_lam):
            b, n, h, d = q.shape
            C = CHUNK
            nc = n // C
            qc = q.reshape(b, nc, C, h, d).transpose(1, 0, 2, 3, 4)
            kc = k.reshape(b, nc, C, h, d).transpose(1, 0, 2, 3, 4)
            vc = v.reshape(b, nc, C, h, d).transpose(1, 0, 2, 3, 4)
            i = jnp.arange(C, dtype=jnp.float32)
            diff = i[:, None] - i[None, :]
            D = jnp.where(diff[None] >= 0, jnp.exp(log_lam[:, None, None] * diff[None]), 0.0)
            decay_q = jnp.exp(log_lam[None, :] * (i[:, None] + 1.0))
            decay_k = jnp.exp(log_lam[None, :] * (C - 1.0 - i[:, None]))
            lam_C = jnp.exp(log_lam * C)

            def step(S, qkv):
                qi, ki, vi = qkv
                scores = jnp.einsum('bthd,bshd->bhts', qi, ki) * D[None]
                o_intra = jnp.einsum('bhts,bshd->bthd', scores, vi)
                o_inter = jnp.einsum('bthd,bhde->bthe', qi * decay_q[None, :, :, None], S)
                S_new = lam_C[None, :, None, None] * S + jnp.einsum('bshd,bshe->bhde', ki * decay_k[None, :, :, None], vi)
                return (S_new, o_intra + o_inter)
            S0 = jnp.zeros((b, h, d, d), q.dtype)
            _, o = jax.lax.scan(step, S0, (qc, kc, vc))
            return o.transpose(1, 0, 2, 3, 4).reshape(b, n, h, d)

        def _gated_group_rmsnorm(o, gate, weight):
            b, n, d = o.shape
            x = o * jax.nn.sigmoid(gate)
            xg = x.reshape(b, n, HEADS, HEAD_DIM)
            ms = jnp.mean(xg * xg, axis=-1, keepdims=True)
            xg = xg * jax.lax.rsqrt(ms + EPS)
            return xg.reshape(b, n, d) * weight
        b, n, d = x.shape
        q = (x @ Wq).reshape(b, n, HEADS, HEAD_DIM)
        k = (x @ Wk).reshape(b, n, HEADS, HEAD_DIM)
        v = (x @ Wv).reshape(b, n, HEADS, HEAD_DIM)
        q = jax.nn.silu(q)
        k = jax.nn.silu(k)
        q = _lrpe_rotate(q)
        k = _lrpe_rotate(k)
        log_lam = _alibi_log_decay(HEADS)
        o = _lightning_attn(q, k, v, log_lam).reshape(b, n, d)
        gate = x @ Wg1 @ Wg2
        o = _gated_group_rmsnorm(o, gate, norm_weight)
        return o @ Wo

    def _L0_ffn_ref(hidden_states, gate_w, Wg, Wu, Wd, sWg, sWu, sWd, shared_gate_w):
        import jax, jax.numpy as jnp
        import numpy as np
        B, S, D = (1, 512, 512)
        F = 128
        E = 16
        K = 4

        def _swiglu(x, wg, wu, wd):
            return jax.nn.silu(x @ wg) * (x @ wu) @ wd
        bsz, seq_len, dim = hidden_states.shape
        flat = hidden_states.reshape(-1, dim)
        T = flat.shape[0]
        router_logits = flat @ gate_w.T
        router_probs = jax.nn.softmax(router_logits.astype(jnp.float32), axis=-1)
        routing_weights, selected_experts = jax.lax.top_k(router_probs, K)
        routing_weights = routing_weights / routing_weights.sum(axis=-1, keepdims=True)
        routing_weights = routing_weights.astype(hidden_states.dtype)
        comb = jnp.sum(jax.nn.one_hot(selected_experts, E, dtype=flat.dtype) * routing_weights[..., None], axis=1)
        mixed = jnp.zeros_like(flat)
        for e in range(E):
            out_e = _swiglu(flat, Wg[e], Wu[e], Wd[e])
            mixed = mixed + comb[:, e:e + 1] * out_e
        shared = _swiglu(flat, sWg, sWu, sWd)
        shared_gate = jax.nn.sigmoid(flat @ shared_gate_w)
        return (mixed + shared * shared_gate).reshape(bsz, seq_len, dim)
    x = L0_attn_x
    xn = _layernorm(x, axis=-1)
    s = _L0_attn_ref(xn, L0_attn_Wq, L0_attn_Wk, L0_attn_Wv, L0_attn_Wo, L0_attn_Wg1, L0_attn_Wg2, L0_attn_norm_weight)
    g = _silu(_L0_ffn_ref(xn, L0_ffn_gate_w, L0_ffn_Wg, L0_ffn_Wu, L0_ffn_Wd, L0_ffn_sWg, L0_ffn_sWu, L0_ffn_sWd, L0_ffn_shared_gate_w))
    x = x + s * g
    return x

_drawn_inputs = setup_inputs


def setup_inputs(seed=0):
    import zlib

    import numpy as np

    out = dict(_drawn_inputs(seed))
    spreads = {'L0_attn_norm_weight': (1.0, 0.6)}
    factors = {'L0_attn_Wq': 8.0,
     'L0_attn_Wk': 8.0,
     'L0_attn_Wv': 8.0,
     'L0_attn_Wo': 8.0,
     'L0_attn_Wg1': 8.0,
     'L0_attn_Wg2': 8.0,
     'L0_ffn_gate_w': 8.0,
     'L0_ffn_Wg': 8.0,
     'L0_ffn_Wu': 8.0,
     'L0_ffn_Wd': 8.0,
     'L0_ffn_sWg': 8.0,
     'L0_ffn_sWu': 8.0,
     'L0_ffn_sWd': 8.0,
     'L0_ffn_shared_gate_w': 8.0}
    for name, (base, spread) in spreads.items():
        noise = np.random.default_rng([zlib.crc32(name.encode()), seed]).standard_normal(out[name].shape)
        drawn = base * np.exp(spread * noise) if base else spread * noise
        out[name] = jnp.asarray(drawn.astype(out[name].dtype))
    for name, factor in factors.items():
        out[name] = (out[name] * factor).astype(out[name].dtype)
    return out
```

```python
import concourse.bass as bass
from concourse import mybir
from contextlib import ExitStack
import numpy as np

F32 = mybir.dt.float32
F16 = mybir.dt.float16
I32 = mybir.dt.int32
ALU = mybir.AluOpType
ACT = mybir.ActivationFunctionType
AXX = mybir.AxisListType.X
ABSMAX = bass.bass_isa.ReduceOp.absmax

P = 128
NB, SEQ, DM = 8, 512, 512
NTOK = NB * SEQ
NT = NTOK // P
TPB = SEQ // P
DC = DM // P
NH, HD = 16, 32
HQ = P // HD
NG = NH // HQ
E, TOPK, FF = 16, 4, 128
NE = E + 1
REG = NTOK + P
CT = NTOK * TOPK // P + E
CTILES = CT + NT
ROWS = E * REG + NTOK + (CT - NTOK * TOPK // P) * P
WEXP = 2 * DC * 2 * FF + 2 * DM
GU = 2 * FF
XS = 256.0
LN_EPS, RMS_EPS = 1e-5, 1e-6
NKIND = 8
NROUTE = 47
NSMALL = 64
SWAP = [(i + HD // 2) % HD for i in range(HD)]

TAB = {}
_at = 0
for _name, _n in (("cos", SEQ), ("sin", SEQ), ("mask", NH * P), ("dk", DM), ("dq", DM), ("lam", NG * P),
                  ("bd", NG * P), ("ident", P), ("region", E), ("tiles", CTILES)):
    TAB[_name] = (_at, _n)
    _at += _n
NTAB = _at


def tables():
    f = np.float32
    t = np.zeros((P, NTAB), f)

    def put(name, a):
        at, n = TAB[name]
        t[:, at:at + n] = np.asarray(a, f).reshape(P, n)

    p = np.arange(P)
    theta = (10000.0 ** (-2.0 * np.arange(HD // 2) / HD)).astype(f)
    ang = np.arange(SEQ, dtype=f)[None, :] * theta[p % (HD // 2)][:, None]
    put("cos", np.cos(ang))
    put("sin", np.sin(ang) * np.where(p % HD < HD // 2, -1, 1)[:, None].astype(f))
    lam = -(2.0 ** (-8.0 * (np.arange(NH) + 1.0) / NH)).astype(f)
    head = np.arange(NG)[None, :] * HQ + np.arange(HQ)[:, None]
    diff = (p[None, :] - p[:, None]).astype(f)
    m = np.where(diff[:, None, None, :] >= 0,
                 np.exp(np.minimum(lam[head][None, :, :, None] * diff[:, None, None, :], 0)), 0)
    put("mask", m)
    lamd = np.repeat(lam, HD)[None, :]
    put("dk", np.exp(lamd * (P - 1.0 - p[:, None]).astype(f)))
    put("dq", np.exp(lamd * (p[:, None] + 1.0).astype(f)))
    same = (p[:, None] // HD == p[None, :] // HD).astype(f)
    put("bd", np.broadcast_to(same[:, None, :], (P, NG, P)))
    put("lam", np.exp(lam[head[p // HD]] * f(P))[:, :, None] * same[:, None, :])
    put("ident", np.eye(P))
    put("region", np.broadcast_to(np.arange(E) * REG + 1, (P, E)))
    put("tiles", np.broadcast_to(np.arange(CTILES), (P, CTILES)))
    h = np.zeros((P, 3 * P), np.float16)
    h[:, :P] = np.eye(P)
    h[:, P:2 * P] = p[:, None] < p[None, :]
    h[:, 2 * P:] = 1
    return t, h


def pass_a_banks():
    order = []
    for j in range(TPB):
        order += [("xh", j), ("xl", j)]
    order += [("small", 0), ("rt", 0)] + [("qk", u) for u in range(2 * NG)] + [("v", j) for j in range(TPB)]
    order += [("rank", 0)]

    def front(c):
        kt = [("kt", c)] if c < TPB - 1 else []
        return [("gate", c)] + kt + [("sc", c, h) for h in range(HQ)]

    def mid(c):
        return [("o", c)] + ([("inter", c)] if c else []) + ([("kv", c)] if c < TPB - 1 else [])

    def back(c):
        return [("oh", c), ("ol", c), ("wo", c)]

    for c in range(TPB):
        order += front(c) + mid(c)
        if c:
            order += back(c - 1)
    order += back(TPB - 1)
    use = {s: (i % 8, i // 8) for i, s in enumerate(order)}
    per_batch = [sum(1 for b, _ in use.values() if b == i) for i in range(8)]
    return use, per_batch


def build(nc, x, wq, wk, wv, wo, w_small, wg2, norm_w, w_gate, w_up, w_down, tab_d, tab16_d, out):
    ctx = ExitStack()
    with ctx:
        def sb(name, shape, dt, where=ctx):
            return where.enter_context(nc.sbuf_tensor(name, shape, dt))

        def sem(name):
            return ctx.enter_context(nc.semaphore(name))

        xg = nc.dram_tensor("expert_rows", [ROWS, 2 * DM], F16, kind="Internal").ap()
        yg = nc.dram_tensor("expert_outputs", [CTILES * P, DM], F32, kind="Internal").ap()
        s_d = nc.dram_tensor("attention_out", [NTOK, DM], F32, kind="Internal").ap()

        bank = [ctx.enter_context(nc.psum_tensor(f"bank{i}", [P, 512], F32)) for i in range(8)]

        def half(i):
            return bank[i][:, :].bitcast(F16)

        tab = sb("tab", [P, NTAB], F32)
        tab16 = sb("tab16", [P, 3 * P], F16)
        ident16, earlier, ones16 = (tab16[:, i * P:(i + 1) * P] for i in range(3))

        def T(name):
            start, n = TAB[name]
            return tab[:, start:start + n]

        slots_all = sb("slots_all", [P, NT * TOPK], I32)
        w_all = sb("w_all", [P, NT * (TOPK + 1)], F32)
        yrows = sb("yrows", [P, NT * TOPK], I32)
        shared_row = sb("shared_row", [1, 1], I32)
        count = sb("count", [P, TPB + 1, E], F32)
        count_i = sb("count_i", [P, E], I32)
        amax = sb("amax", [P, NKIND], F32)
        amax_all = sb("amax_all", [P, NKIND], F32)
        bits = sb("bits", [P, NKIND], I32)
        sc_i = sb("sc_i", [P, NKIND], I32)
        inv_i = sb("inv_i", [P, NKIND], I32)
        inv_x = sb("inv_x", [P, NKIND], F32)
        am_new = sb("am_new", [P, 3], F32)
        neg_half = sb("neg_half", [P, NH], F32)

        def scale_of(k):
            return sc_i[:, k:k + 1].bitcast(F32)

        a = ExitStack()
        w16 = {n: sb(f"w16_{n}", [P, 2, DC, DM], F16, a) for n in "qkvo"}
        ws16 = sb("ws16", [P, 2, DC, NSMALL], F16, a)
        wg2_sb = sb("wg2_sb", [2 * HD, DM], F32, a)
        nw = sb("nw", [P, DC], F32, a)
        stage = sb("stage", [P, 4, DC * DM], F32, a)
        raw_small = sb("raw_small", [P, DC * NSMALL], F32, a)
        x_t = sb("x_t", [P, TPB, DM], F32, a)
        stats = sb("stats", [P, TPB, 6], F32, a)
        mv = sb("mv", [P, TPB, 2], F32, a)
        var_eps = sb("var_eps", [P, TPB], F32, a)
        rstd = sb("rstd", [P, TPB], F32, a)
        xs = sb("xs", [P, 2, DM], F32, a)
        x16 = sb("x16", [P, TPB, 2 * DM], F16, a)
        xT = sb("xT", [P, 2, DC, SEQ], F16, a)
        gT = sb("gT", [NSMALL, SEQ], F32, a)
        lg = sb("lg", [P, TPB, E + 1], F32, a)
        mx = sb("mx", [P, TPB, 1], F32, a)
        delta = sb("delta", [P, TPB, E + 1], F32, a)
        pp = sb("pp", [P, TPB, E + TOPK], F32, a)
        sgx = sb("sgx", [P, TPB, 1], F32, a)
        sgy = sb("sgy", [P, TPB, 1], F32, a)
        m8 = sb("m8", [P, TPB, 8], F32, a)
        msel = sb("msel", [P, TPB, 8], F32, a)
        marked = sb("marked", [P, TPB, E + TOPK], F32, a)
        chosen = sb("chosen", [P, TPB, E], F16, a)
        wsum = sb("wsum", [P, TPB, 1], F32, a)
        wrec = sb("wrec", [P, TPB, 1], F32, a)
        comb0 = sb("comb0", [P, TPB, E], F32, a)
        comb = sb("comb", [P, TPB, E], F32, a)
        slot0 = sb("slot0", [P, TPB, E], F32, a)
        slot1 = sb("slot1", [P, TPB, E], F32, a)
        key = sb("key", [P, TPB, E], F32, a)
        k8 = sb("k8", [P, TPB, 8], F32, a)
        slots = sb("slots", [P, TPB, TOPK], I32, a)
        wtok = sb("wtok", [P, TPB, TOPK + 1], F32, a)
        junk = sb("junk", [P, TPB * TOPK, E], F32, a)
        qs = sb("qs", [P, 2, SEQ], F32, a)
        qswap = sb("qswap", [P, SEQ], F32, a)
        qsin = sb("qsin", [P, SEQ], F32, a)
        qcos = sb("qcos", [P, 2, SEQ], F32, a)
        qkT = sb("qkT", [P, 2 * NG, SEQ], F32, a)
        raw_last = qkT[:, 0:3, :]
        v_sb = sb("v_sb", [P, TPB, DM], F32, a)
        sig = sb("sig", [P, 2, DM], F32, a)
        kd = sb("kd", [P, DM], F32, a)
        probs = sb("probs", [P, HQ, NG * P], F32, a)
        state = sb("state", [P, NG * P], F32, a)
        state_in = sb("state_in", [P, NG * P], F32, a)
        inter = sb("inter", [P, DM], F32, a)
        o_sum = sb("o_sum", [P, DM], F32, a)
        og = sb("og", [P, 2, DM], F32, a)
        sq = sb("sq", [P, DM], F32, a)
        ms = sb("ms", [P, NH], F32, a)
        ms_eps = sb("ms_eps", [P, NH], F32, a)
        rms = sb("rms", [P, NH], F32, a)
        on = sb("on", [P, DM], F32, a)
        o16 = sb("o16", [P, 2 * DM], F16, a)
        oT = sb("oT", [P, 2, DC, P], F16, a)
        s_sb = sb("s_sb", [P, 2, DM], F32, a)
        zeros = sb("zeros", [P, 2 * DM], F16, a)
        a.close()

        c_ = ExitStack()
        we = sb("we", [P, NE * WEXP], F16, c_)
        raw = sb("raw", [P, 2, 3, DM], F32, c_)
        xin = sb("xin", [P, 4, 2 * DM], F16, c_)
        xTc = sb("xTc", [P, 2, 2, DC, P], F16, c_)
        sg = sb("sg", [P, 2, FF], F32, c_)
        hf = sb("hf", [P, 2, FF], F32, c_)
        h16 = sb("h16", [P, 2, 2, FF], F16, c_)
        hT = sb("hT", [P, 2, 2, P], F16, c_)
        y_sb = sb("y_sb", [P, 4, DM], F32, c_)
        tcnt = sb("tcnt", [P, E], F32, c_)
        tiles_i = sb("tiles_i", [P, E], I32, c_)
        tsum = sb("tsum", [P, 5, E], F32, c_)
        shift = sb("shift", [P, E], F32, c_)
        slots_f = sb("slots_f", [P, NT * TOPK], F32, c_)
        moved = sb("moved", [P, NT * TOPK], F32, c_)
        ysum = sb("ysum", [P, NT * TOPK], F32, c_)
        ge = sb("ge", [1, CTILES], F32, c_)
        expert_f = sb("expert_f", [1, CTILES], F32, c_)
        before_f = sb("before_f", [1, CTILES], F32, c_)
        local_f = sb("local_f", [1, CTILES], F32, c_)
        rowbase_f = sb("rowbase_f", [1, CTILES], F32, c_)
        row_i = sb("row_i", [1, CTILES], I32, c_)
        off_i = sb("off_i", [1, CTILES], I32, c_)
        csc = sb("csc", [P, 4], F32, c_)
        c_.close()

        d_ = ExitStack()
        ygat = sb("ygat", [P, 2, TOPK, DM], F32, d_)
        idx = sb("idx", [P, 2, TOPK], I32, d_)
        wd5 = sb("wd5", [P, 2, TOPK + 1], F32, d_)
        ysh = sb("ysh", [P, 2, DM], F32, d_)
        x_d = sb("x_d", [P, 2, DM], F32, d_)
        s_x = sb("s_x", [P, 2, DM], F32, d_)
        acc = sb("acc", [P, 2, TOPK + 1, DM], F32, d_)
        gate_s = sb("gate_s", [P, 2, DM], F32, d_)
        prod = sb("prod", [P, 2, DM], F32, d_)
        res = sb("res", [P, 2, DM], F32, d_)
        d_.close()

        LOOP = {}

        def lsem(name, n):
            LOOP[name] = (sem(name), n)
            return name

        USE, UPB = pass_a_banks()
        for i in range(8):
            lsem(f"bank{i}_full", UPB[i])
        for j in range(TPB):
            lsem(f"x_in{j}", 16)
        for name, n in dict(
                stat_done=TPB, mv_ready=TPB, vareps_ready=TPB, rstd_ready=TPB, xs_ready=TPB,
                xhi_ready=TPB, xlo_ready=TPB, xTh_ready=TPB, xTl_ready=TPB, xrow_out=16 * TPB,
                gT_ready=1, logits_ready=1, max_ready=1, delta_ready=2, exp_ready=2, route=NROUTE,
                chosen_ready=1, rank_read=1, slots_ready=1, rows_sent=1,
                qs_ready=2 * NG, swap_done=2 * NG, sin_done=2 * NG, cos_done=2 * NG, qk_ready=2 * NG,
                v_ready=TPB, sig_ready=TPB, kd_ready=TPB - 1, probs_ready=TPB * HQ, inter_done=TPB - 1,
                osum_done=TPB, og_ready=TPB, kv_read=TPB - 1, state_decayed=TPB - 2, state_ready=TPB - 1,
                sq_ready=TPB, ms_ready=TPB, mseps_ready=TPB, rms_ready=TPB, on_ready=TPB,
                ohi_ready=TPB, olo_ready=TPB, oTh_ready=TPB, oTl_ready=TPB, s_ready=TPB, s_out0=8 * TPB, s_out1=8 * TPB,
                raw_in=16 * 5, raw_max=3, am_ready=1).items():
            lsem(name, n)

        def S(name):
            return LOOP[name][0]

        def at(name, b, m):
            n = LOOP[name][1]
            return b * n + (n + m)

        def wait(eng, name, b, m):
            eng.wait_ge(S(name), at(name, b, m))

        def apart(eng):
            eng.nop(nofuse=True)

        def full(stage):
            return S(f"bank{USE[stage][0]}_full")

        def filled(eng, b, *stage, row=0):
            i, k = USE[stage]
            wait(eng, f"bank{i}_full", b, k + 1 + row * UPB[i])

        READER = {}
        for j in range(TPB):
            READER["xh", j] = ("xTh_ready", j + 1)
            READER["xl", j] = ("xTl_ready", j + 1)
            READER["v", j] = ("v_ready", j + 1)
            READER["gate", j] = ("sig_ready", j + 1)
            READER["kt", j] = ("kd_ready", j + 1)
            READER["o", j] = ("osum_done", j + 1)
            READER["inter", j] = ("inter_done", j)
            READER["kv", j] = ("kv_read", j + 1)
            READER["oh", j] = ("oTh_ready", j + 1)
            READER["ol", j] = ("oTl_ready", j + 1)
            READER["wo", j] = ("s_ready", j + 1)
            for h in range(HQ):
                READER["sc", j, h] = ("probs_ready", j * HQ + h + 1)
        for u in range(2 * NG):
            READER["qk", u] = ("qs_ready", u + 1)
        READER["small", 0] = ("gT_ready", 1)
        READER["rt", 0] = ("logits_ready", 1)
        READER["rank", 0] = ("rank_read", 1)
        BEFORE = {}
        for i in range(8):
            mine = sorted((s for s in USE if USE[s][0] == i), key=lambda s: USE[s][1])
            for n, s in enumerate(mine):
                BEFORE[s] = (mine[n - 1], -1 if n == 0 else 0)

        def emptied(eng, b, *stage):
            before, row = BEFORE[stage]
            name, m = READER[before]
            wait(eng, name, b, m + row * LOOP[name][1])

        scattered = sem("scattered")
        tab_in = sem("tab_in")
        w_in = [sem(f"w_in_{n}") for n in "qkvo"]
        small_in = sem("small_in")
        last_in = sem("last_in")
        const_pool = sem("const_pool")
        const_dve = sem("const_dve")
        fold_done = sem("fold_done")
        amax_ready = sem("amax_ready")
        amax_done = sem("amax_done")
        scale_chain = sem("scale_chain")
        scale_ready = sem("scale_ready")
        whi_ready = sem("whi_ready")
        wlo_ready = sem("wlo_ready")
        zero_rows = sem("zero_rows")
        counts_ready = sem("counts_ready")
        a_done = sem("a_done")
        emax_done = sem("emax_done")
        cchain = sem("cchain")
        csc_ready = sem("csc_ready")
        meta_ready = sem("meta_ready")
        e_in = [sem(f"e_in{i}") for i in range(2)]
        e_hi = sem("e_hi")
        e_lo = sem("e_lo")
        xin_ready = [sem(f"xin_ready{i}") for i in range(4)]
        turned = sem("turned")
        xTc_hi = sem("xTc_hi")
        xTc_lo = sem("xTc_lo")
        gu_done = sem("gu_done")
        sg_ready = sem("sg_ready")
        h_ready = sem("h_ready")
        h_hi = sem("h_hi")
        h_lo = sem("h_lo")
        h_turned = sem("h_turned")
        hT_ready = sem("hT_ready")
        y_done = sem("y_done")
        y_ready = sem("y_ready")
        y_out = [sem(f"y_out{i}") for i in range(4)]
        c_done = sem("c_done")
        idx_ready = sem("idx_ready")
        gathered = [sem(f"gathered{i}") for i in range(2)]
        d_in = [sem(f"d_in{i}") for i in range(2)]
        acc_done = sem("acc_done")
        silu_done = sem("silu_done")
        prod_done = sem("prod_done")
        res_ready = sem("res_ready")
        res_out = [sem(f"res_out{i}") for i in range(2)]

        def contract_rows(w):
            return w.rearrange("(c p) n -> p c n", p=P)

        gate_v = w_gate.rearrange("e (c p) n -> e p c n", p=P)
        up_v = w_up.rearrange("e (c p) n -> e p c n", p=P)

        def credit(eng, names):
            for name in names:
                eng.sem_inc(S(name), LOOP[name][1])

        def barrier(eng, s):
            eng.drain().then_inc(s, 1)
            eng.wait_ge(s, 5)

        def pair3(lhs, rhs, n):
            return [(lhs(a_, c), rhs(b_, c)) for c in range(n) for a_, b_ in ((0, 0), (0, 1), (1, 0))]

        def sum_products(eng, dst, pairs):
            for n, (lhsT, rhs) in enumerate(pairs):
                last = eng.matmul(dst, lhsT, rhs, start=(n == 0), stop=(n == len(pairs) - 1))
            return last

        block = ctx.enter_context(nc.Block())
        NC4 = CTILES // 4
        XH, XL, HT, GUB, YB = 0, 1, 2, 3, 5

        @block.sync
        def _(sp):
            credit(sp, [f"x_in{j}" for j in range(TPB)] + ["xrow_out", "s_out0", "s_out1", "raw_in"])
            sp.dma_start(tab[:, :], tab_d).then_inc(tab_in, 16)
            sp.dma_start(tab16[:, :], tab16_d).then_inc(tab_in, 16)
            sp.dma_start(nw[:, :], norm_w.rearrange("(c p) -> p c", p=P),
                         allow_slow_non_contiguous=True).then_inc(tab_in, 16)
            sp.dma_start(wg2_sb[HD:2 * HD, :], wg2).then_inc(tab_in, 16)
            for i, w in enumerate((wq, wk, wv, wo)):
                sp.dma_start(stage[:, i, :].rearrange("p (c n) -> p c n", c=DC),
                             contract_rows(w)).then_inc(w_in[i], 16)
            sp.dma_start(raw_small[:, :].rearrange("p (c n) -> p c n", c=DC),
                         contract_rows(w_small)).then_inc(small_in, 16)
            for k, v in enumerate((gate_v[E], up_v[E])):
                sp.dma_start(raw_last[:, k, :].rearrange("p (c n) -> p c n", c=DC), v).then_inc(last_in, 16)
            sp.dma_start(raw_last[:, 2, :], w_down[E]).then_inc(last_in, 16)
            sp.wait_ge(const_pool, 1)
            for i in range((ROWS - E * REG - NTOK) // P):
                sp.dma_start(xg[E * REG + NTOK + i * P:E * REG + NTOK + (i + 1) * P, :],
                             zeros[:, :]).then_inc(zero_rows, 16)
            sp.wait_ge(wlo_ready, 5)
            sp.wait_ge(whi_ready, 5)
            with sp.Fori(0, NB) as b:
                wait(sp, "raw_max", b, 0)
                for i in range(2):
                    for k, v in enumerate((gate_v, up_v)):
                        sp.dma_start(stage[:, k, i * DM:(i + 1) * DM].rearrange("p (o c n) -> p o c n", o=1, c=DC),
                                     v[bass.ds(b * 2 + i, 1)].rearrange("o p c n -> p o c n")).then_inc(S("raw_in"), 16)
                sp.dma_start(stage[:, 2, 0:2 * DM].rearrange("p (o n) -> p o n", o=2),
                             w_down[bass.ds(b * 2, 2)].rearrange("o p n -> p o n")).then_inc(S("raw_in"), 16)
                for j in range(TPB):
                    wait(sp, "xs_ready", b, j + 1 - TPB)
                    sp.dma_start(x_t[:, j, :], x[bass.ds(b * SEQ + j * P, P), :]).then_inc(S(f"x_in{j}"), 16)
                for j in range(TPB):
                    wait(sp, "xhi_ready", b, j + 1)
                    wait(sp, "xlo_ready", b, j + 1)
                    sp.dma_start(xg[bass.ds(b * SEQ + (E * REG + j * P), P), :],
                                 x16[:, j, :]).then_inc(S("xrow_out"), 16)
                for c in range(TPB):
                    wait(sp, "s_ready", b, c + 1)
                    sp.dma_start(s_d[bass.ds(b * SEQ + c * P, P), :],
                                 s_sb[:, c % 2, :]).then_inc(S(f"s_out{c % 2}"), 16)
            sp.wait_ge(counts_ready, 1)
            for e in range(E):
                n = sp.value_load(count_i[0:1, e:e + 1], min_val=0, max_val=NTOK)
                sp.dma_start(xg[bass.ds(n + e * REG, P), :], zeros[:, :]).then_inc(zero_rows, 16)
            sp.wait_ge(zero_rows, 16 * (E + (ROWS - E * REG - NTOK) // P))
            wait(sp, "s_out0", NB - 1, 8 * TPB)
            wait(sp, "s_out1", NB - 1, 8 * TPB)
            wait(sp, "xrow_out", NB - 1, 16 * TPB)
            barrier(sp, a_done)

            def load_expert(e, i):
                for k, v in enumerate((gate_v, up_v)):
                    sp.dma_start(raw[:, i, k, :].rearrange("p (o c n) -> p o c n", o=1, c=DC),
                                 v[bass.ds(e, 1)].rearrange("o p c n -> p o c n")).then_inc(e_in[i], 16)
                sp.dma_start(raw[:, i, 2, :].rearrange("p (o n) -> p o n", o=1),
                             w_down[bass.ds(e, 1)].rearrange("o p n -> p o n")).then_inc(e_in[i], 16)

            load_expert(0, 0)
            load_expert(1, 1)
            with sp.Fori(1, E // 2) as e2:
                for i in range(2):
                    sp.wait_ge(e_hi, e2 * 6 + (3 * i - 3))
                    sp.wait_ge(e_lo, e2 * 6 + (3 * i - 3))
                    load_expert(e2 * 2 + i, i)
            sp.wait_ge(e_hi, 3 * (E - 1))
            sp.wait_ge(e_lo, 3 * (E - 1))
            load_expert(E, 0)

            for k in range(4):
                sp.sem_inc(y_out[k], 16)
            sp.wait_ge(meta_ready, 2)

            def load_rows(t, k, first=False):
                row = sp.value_load(row_i[0:1, bass.ds(t, 1)], min_val=0, max_val=ROWS - P)
                if not first:
                    sp.wait_ge(turned, t - 3)
                sp.dma_start(xin[:, k, :], xg[bass.ds(row, P), :]).then_inc(xin_ready[k], 16)

            def store_rows(t, k):
                sp.wait_ge(y_ready, t + 1)
                sp.dma_start(yg[bass.ds(t * P, P), :], y_sb[:, k, :]).then_inc(y_out[k], 16)

            for k in range(4):
                load_rows(k, k, first=True)
            with sp.Fori(0, NC4 - 1) as g:
                for k in range(4):
                    load_rows(g * 4 + (k + 4), k)
                    store_rows(g * 4 + k, k)
            for k in range(4):
                store_rows(CTILES - 4 + k, k)
            for k in range(4):
                sp.wait_ge(y_out[k], 16 * (NC4 + 1))
            barrier(sp, c_done)

            shared = sp.value_load(shared_row[0:1, 0:1], min_val=0, max_val=CT * P)

            def load_d(i, k):
                sp.dma_start(x_d[:, k, :], x[bass.ds(i * P, P), :]).then_inc(d_in[k], 16)
                sp.dma_start(s_x[:, k, :], s_d[bass.ds(i * P, P), :]).then_inc(d_in[k], 16)
                sp.dma_start(ysh[:, k, :], yg[bass.ds(shared + i * P, P), :]).then_inc(d_in[k], 16)

            def store_d(i, k):
                sp.wait_ge(res_ready, i + 1)
                sp.dma_start(out[bass.ds(i * P, P), :], res[:, k, :]).then_inc(res_out[k], 16)

            for k in range(2):
                load_d(k, k)
            with sp.Fori(0, NT // 2 - 1) as g:
                for k in range(2):
                    store_d(g * 2 + k, k)
                    load_d(g * 2 + (k + 2), k)
            for k in range(2):
                store_d(NT - 2 + k, k)
            for k in range(2):
                sp.wait_ge(res_out[k], 16 * NT // 2)

        @block.gpsimd
        def _(pool):
            credit(pool, ["vareps_ready", "rstd_ready", "xlo_ready", "cos_done", "rows_sent",
                          "mseps_ready", "rms_ready", "olo_ready"])
            pool.memset(zeros[:, :], 0.0).then_inc(const_pool, 1)
            pool.memset(neg_half[:, :], -0.5).then_inc(const_pool, 1)
            pool.wait_ge(amax_ready, 5)
            pool.partition_all_reduce(amax_all[:, 0:5], amax[:, 0:5], P, ABSMAX).then_inc(amax_done, 1)
            pool.wait_ge(tab_in, 64)
            pool.wait_ge(const_pool, 2)
            with pool.Fori(0, NB) as b:
                def rsqrt_var(j):
                    wait(pool, "mv_ready", b, j + 1)
                    apart(pool)
                    pool.tensor_scalar(var_eps[:, j:j + 1], mv[:, j, 1:2], LN_EPS, 1 / XS ** 2, ALU.add,
                                       ALU.mult).then_inc(S("vareps_ready"), 1)
                    wait(pool, "vareps_ready", b, j + 1)
                    pool.tensor_tensor(rstd[:, j:j + 1], var_eps[:, j:j + 1], neg_half[:, 0:1],
                                       ALU.pow).then_inc(S("rstd_ready"), 1)

                def low(j):
                    wait(pool, "xs_ready", b, j + 1)
                    wait(pool, "xhi_ready", b, j + 1)
                    filled(pool, b, "xl", j, row=-1)
                    if j == 0:
                        wait(pool, "rows_sent", b, 0)
                        wait(pool, "xrow_out", b, 0)
                    pool.tensor_tensor(x16[:, j, DM:2 * DM], xs[:, j % 2, :], x16[:, j, 0:DM],
                                       ALU.subtract).then_inc(S("xlo_ready"), 1)

                rsqrt_var(0)
                rsqrt_var(1)
                low(0)
                rsqrt_var(2)
                low(1)
                rsqrt_var(3)
                low(2)
                low(3)
                for u in range(2 * NG):
                    wait(pool, "qs_ready", b, u + 1)
                    wait(pool, "qk_ready", b, u - 1)
                    pool.tensor_tensor(qcos[:, u % 2, :], qs[:, u % 2, :], T("cos"),
                                       ALU.mult).then_inc(S("cos_done"), 1)

                def rsqrt_ms(c):
                    wait(pool, "ms_ready", b, c + 1)
                    apart(pool)
                    pool.tensor_scalar(ms_eps[:, :], ms[:, :], 1 / (HD * XS ** 2), RMS_EPS / XS ** 2,
                                       ALU.mult, ALU.add).then_inc(S("mseps_ready"), 1)
                    wait(pool, "mseps_ready", b, c + 1)
                    wait(pool, "on_ready", b, c)
                    pool.tensor_tensor(rms[:, :], ms_eps[:, :], neg_half[:, :],
                                       ALU.pow).then_inc(S("rms_ready"), 1)

                for c in range(TPB):
                    rsqrt_ms(c)
                    wait(pool, "on_ready", b, c + 1)
                    wait(pool, "ohi_ready", b, c + 1)
                    filled(pool, b, "ol", (c - 1) % TPB, row=-1 if c == 0 else 0)
                    pool.tensor_tensor(o16[:, DM:2 * DM], on[:, :], o16[:, 0:DM],
                                       ALU.subtract).then_inc(S("olo_ready"), 1)
                    if c == 0:
                        wait(pool, "slots_ready", b, 1)
                        apart(pool)
                    for k in range(TOPK):
                        pool.indirect_dma_start(
                            out=xg, out_offset=bass.IndirectOffsetOnAxis(ap=slots[:, c, k:k + 1], axis=0),
                            in_=x16[:, c, :], in_offset=None).then_inc(scattered, 16)
                pool.wait_ge(scattered, b * (16 * TPB * TOPK) + 16 * TPB * TOPK)
                pool.sem_inc(S("rows_sent"), 1)
            wait(pool, "am_ready", NB - 1, 1)
            pool.partition_all_reduce(amax_all[:, 5:8], amax[:, 5:8], P, ABSMAX).then_inc(emax_done, 1)
            pool.wait_ge(emax_done, 1)
            barrier(pool, a_done)
            barrier(pool, c_done)

            def gather(i, k):
                pool.wait_ge(idx_ready, i + 1)
                apart(pool)
                for n in range(TOPK):
                    pool.indirect_dma_start(
                        out=ygat[:, k, n, :], out_offset=None, in_=yg,
                        in_offset=bass.IndirectOffsetOnAxis(ap=idx[:, k, n:n + 1], axis=0),
                    ).then_inc(gathered[k], 16)

            with pool.Fori(0, NT // 2) as g:
                for k in range(2):
                    gather(g * 2 + k, k)

        @block.scalar
        def _(act):
            credit(act, ["xhi_ready", "xTh_ready", "gT_ready", "exp_ready", "qs_ready", "v_ready",
                         "sig_ready", "sq_ready", "ohi_ready", "oTh_ready", "s_ready"])
            act.wait_ge(scale_ready, 1)
            for i, name in enumerate("qkvo"):
                act.activation(w16[name][:, 0, :, :].rearrange("p c n -> p (c n)"), stage[:, i, :], ACT.Copy,
                               scale=scale_of(i)).then_inc(whi_ready, 1)
            act.activation(ws16[:, 0, :, :].rearrange("p c n -> p (c n)"), raw_small[:, :], ACT.Copy,
                           scale=scale_of(4)).then_inc(whi_ready, 1)

            def ix(k):
                return inv_x[:, k:k + 1]

            with act.Fori(0, NB) as b:
                def high(j):
                    wait(act, "xs_ready", b, j + 1)
                    if j == 0:
                        wait(act, "rows_sent", b, 0)
                        wait(act, "xrow_out", b, 0)
                    act.activation(x16[:, j, 0:DM], xs[:, j % 2, :], ACT.Copy).then_inc(S("xhi_ready"), 1)

                def turn_high(j):
                    filled(act, b, "xh", j)
                    if j == 0:
                        filled(act, b, "v", TPB - 1, row=-1)
                    act.activation(xT[:, 0, :, j * P:(j + 1) * P],
                                   half(USE["xh", j][0])[:, 0:DM].rearrange("p (c n) -> p c n", c=DC),
                                   ACT.Copy).then_inc(S("xTh_ready"), 1)

                high(0)
                high(1)
                turn_high(0)
                high(2)
                turn_high(1)
                high(3)
                turn_high(2)
                turn_high(3)
                filled(act, b, "small", 0)
                filled(act, b, "gate", TPB - 1, row=-1)
                act.activation(gT[:, :], bank[USE["small", 0][0]][0:NSMALL, :], ACT.Copy,
                               scale=inv_x[0:NSMALL, 4:5]).then_inc(S("gT_ready"), 1)

                def silu_qk(u):
                    filled(act, b, "qk", u)
                    wait(act, "swap_done", b, u - 1)
                    wait(act, "cos_done", b, u - 1)
                    act.activation(qs[:, u % 2, :], bank[USE["qk", u][0]][:, :], ACT.Silu,
                                   scale=ix(u // NG)).then_inc(S("qs_ready"), 1)

                for u in range(2 * NG):
                    silu_qk(u)
                    if u == 1:
                        wait(act, "delta_ready", b, 2)
                        act.activation(pp[:, :, 0:E], delta[:, :, 0:E], ACT.Exp).then_inc(S("exp_ready"), 1)
                        act.activation(sgx[:, :, :], delta[:, :, E:E + 1], ACT.Exp).then_inc(S("exp_ready"), 1)
                for j in range(TPB):
                    filled(act, b, "v", j)
                    if j == 0:
                        filled(act, b, "o", TPB - 1, row=-1)
                        filled(act, b, "kv", TPB - 2, row=-1)
                    act.activation(v_sb[:, j, :], bank[USE["v", j][0]][:, :], ACT.Copy,
                                   scale=ix(2)).then_inc(S("v_ready"), 1)

                def gates(c):
                    filled(act, b, "gate", c)
                    wait(act, "og_ready", b, c - 1)
                    act.activation(sig[:, c % 2, :], bank[USE["gate", c][0]][:, :],
                                   ACT.Sigmoid).then_inc(S("sig_ready"), 1)

                def squares(c):
                    wait(act, "og_ready", b, c + 1)
                    wait(act, "ms_ready", b, c)
                    act.activation(sq[:, :], og[:, c % 2, :], ACT.Square).then_inc(S("sq_ready"), 1)

                def high_o(c):
                    wait(act, "on_ready", b, c + 1)
                    filled(act, b, "oh", (c - 1) % TPB, row=-1 if c == 0 else 0)
                    wait(act, "olo_ready", b, c)
                    act.activation(o16[:, 0:DM], on[:, :], ACT.Copy).then_inc(S("ohi_ready"), 1)

                def finish(c):
                    filled(act, b, "oh", c)
                    filled(act, b, "wo", (c - 1) % TPB, row=-1 if c == 0 else 0)
                    act.activation(oT[:, 0, :, :],
                                   half(USE["oh", c][0])[:, 0:DM].rearrange("p (c n) -> p c n", c=DC),
                                   ACT.Copy).then_inc(S("oTh_ready"), 1)
                    filled(act, b, "wo", c)
                    wait(act, f"s_out{c % 2}", b, 16 * (c // 2))
                    act.activation(s_sb[:, c % 2, :], bank[USE["wo", c][0]][:, :], ACT.Copy,
                                   scale=ix(3)).then_inc(S("s_ready"), 1)

                for c in range(TPB):
                    gates(c)
                    if c:
                        high_o(c - 1)
                    squares(c)
                    if c:
                        finish(c - 1)
                high_o(TPB - 1)
                finish(TPB - 1)
            barrier(act, a_done)

            act.wait_ge(csc_ready, 1)

            def split_high(e, i):
                act.wait_ge(e_in[i], e * 24 + (48 - 24 * i))
                for k in range(3):
                    act.activation(expert_part(we, e, 0, k), raw_part(raw, i, k), ACT.Copy,
                                   scale=scale_of(5 + k)).then_inc(e_hi, 1)

            with act.Fori(0, E // 2) as e2:
                for i in range(2):
                    split_high(e2 * 2 + i, i)
            split_high(E, 0)

            def x_high(t, k):
                act.wait_ge(turned, t + 1)
                act.activation(xTc[:, k % 2, 0, :, :],
                               half(XH)[:, 0:DM].rearrange("p (c n) -> p c n", c=DC),
                               ACT.Copy).then_inc(xTc_hi, 1)

            def silu_gate(t, k):
                act.wait_ge(gu_done, t + 1)
                act.activation(sg[:, k % 2, :], bank[GUB + k % 2][:, 0:FF], ACT.Silu,
                               scale=inv_x[:, 5:6]).then_inc(sg_ready, 1)

            def h_high(t, k):
                act.wait_ge(h_ready, t + 1)
                act.activation(h16[:, k % 2, 0, :], hf[:, k % 2, :], ACT.Copy).then_inc(h_hi, 1)

            def y_read(t, k):
                act.wait_ge(y_done, t + 1)
                act.wait_ge(y_out[k], t * 4 + (16 - 4 * k))
                act.activation(y_sb[:, k, :], bank[YB + k % 2][:, :], ACT.Copy,
                               scale=csc[:, 1:2]).then_inc(y_ready, 1)

            def tiles_of(base, first=False, last=False):
                for k in range(4):
                    t = base + k
                    silu_gate(t, k)
                    if not (last and k == 3):
                        x_high(t + 1, (k + 1) % 4)
                    if not (first and k == 0):
                        y_read(t - 1, (k - 1) % 4)
                    h_high(t, k)

            x_high(0, 0)
            tiles_of(0, first=True)
            with act.Fori(1, NC4 - 1) as g:
                tiles_of(g * 4)
            tiles_of(CTILES - 4, last=True)
            y_read(CTILES - 1, 3)
            barrier(act, c_done)

            def silu_d(i, k):
                act.wait_ge(acc_done, i * (TOPK + 1) + (TOPK + 1))
                act.activation(gate_s[:, k, :], acc[:, k, TOPK, :], ACT.Silu).then_inc(silu_done, 1)

            with act.Fori(0, NT // 2) as g:
                for k in range(2):
                    silu_d(g * 2 + k, k)

        @block.vector
        def _(dve):
            credit(dve, ["stat_done", "mv_ready", "xs_ready", "xTl_ready", "logits_ready", "max_ready",
                         "delta_ready", "route", "chosen_ready", "rank_read", "slots_ready", "swap_done",
                         "sin_done", "qk_ready", "kd_ready", "probs_ready", "inter_done", "osum_done",
                         "og_ready", "kv_read", "state_decayed", "state_ready", "ms_ready", "on_ready",
                         "oTl_ready", "raw_max", "am_ready"])
            dve.memset(pp[:, :, E:E + TOPK], -1.0).then_inc(const_dve, 1)
            dve.memset(msel[:, :, TOPK:8], -1.0).then_inc(const_dve, 1)
            dve.memset(count[:, :, :], 0.0).then_inc(const_dve, 1)
            dve.wait_ge(tab_in, 64)
            dve.wait_ge(w_in[3], 16)
            for c in range(DC):
                dve.tensor_scalar(stage[:, 3, c * DM:(c + 1) * DM], stage[:, 3, c * DM:(c + 1) * DM],
                                  nw[:, c:c + 1], None, ALU.mult).then_inc(fold_done, 1)
            for i in range(3):
                dve.wait_ge(w_in[i], 16)
                dve.tensor_reduce(amax[:, i:i + 1], stage[:, i, :], AXX, ALU.max,
                                  apply_absolute_value=True).then_inc(amax_ready, 1)
            dve.wait_ge(fold_done, DC)
            dve.tensor_reduce(amax[:, 3:4], stage[:, 3, :], AXX, ALU.max,
                              apply_absolute_value=True).then_inc(amax_ready, 1)
            dve.wait_ge(small_in, 16)
            dve.tensor_reduce(amax[:, 4:5], raw_small[:, :], AXX, ALU.max,
                              apply_absolute_value=True).then_inc(amax_ready, 1)
            dve.wait_ge(last_in, 48)
            dve.tensor_reduce(amax[:, 5:8], raw_last[:, :, :], AXX, ALU.max,
                              apply_absolute_value=True).then_inc(amax_ready, 1)

            def powers(lo, hi, chain, n):
                k = slice(lo, hi)
                dve.tensor_scalar(amax_all[:, k], amax_all[:, k], 2.0 ** -60, None, ALU.max).then_inc(chain, 1)
                dve.wait_ge(chain, n + 1)
                dve.tensor_scalar(bits[:, k], amax_all[:, k].bitcast(I32), 0x7F800000, None,
                                  ALU.bitwise_and).then_inc(chain, 1)
                dve.wait_ge(chain, n + 2)
                dve.tensor_scalar(sc_i[:, k], bits[:, k], -1.0, float(268 << 23), ALU.mult,
                                  ALU.add).then_inc(chain, 1)
                dve.wait_ge(chain, n + 3)
                dve.tensor_scalar(inv_i[:, k], sc_i[:, k], -1.0, float(254 << 23), ALU.mult,
                                  ALU.add).then_inc(chain, 1)
                dve.wait_ge(chain, n + 4)

            dve.wait_ge(amax_done, 1)
            powers(0, 5, scale_chain, 0)
            dve.tensor_scalar(inv_x[:, 0:5], inv_i[:, 0:5].bitcast(F32), 1 / XS, None,
                              ALU.mult).then_inc(scale_ready, 1)
            for i, name in enumerate("qkvo"):
                dve.wait_ge(whi_ready, i + 1)
                dve.scalar_tensor_tensor(w16[name][:, 1, :, :].rearrange("p c n -> p (c n)"), stage[:, i, :],
                                         scale_of(i), w16[name][:, 0, :, :].rearrange("p c n -> p (c n)"),
                                         ALU.mult, ALU.subtract).then_inc(wlo_ready, 1)
            dve.wait_ge(whi_ready, 5)
            dve.scalar_tensor_tensor(ws16[:, 1, :, :].rearrange("p c n -> p (c n)"), raw_small[:, :],
                                     scale_of(4), ws16[:, 0, :, :].rearrange("p c n -> p (c n)"),
                                     ALU.mult, ALU.subtract).then_inc(wlo_ready, 1)
            dve.wait_ge(const_dve, 3)
            dve.wait_ge(amax_ready, 6)

            with dve.Fori(0, NB) as b:
                def moments(j):
                    wait(dve, f"x_in{j}", b, 16)
                    wait(dve, "mv_ready", b, j + 1 - TPB)
                    dve.bn_stats(stats[:, j, :], x_t[:, j, :]).then_inc(S("stat_done"), 1)
                    wait(dve, "stat_done", b, j + 1)
                    wait(dve, "rstd_ready", b, j + 1 - TPB)
                    apart(dve)
                    dve.bn_aggr(mv[:, j, :], stats[:, j, :]).then_inc(S("mv_ready"), 1)

                def normalize(j):
                    wait(dve, "rstd_ready", b, j + 1)
                    wait(dve, "xhi_ready", b, j - 1)
                    wait(dve, "xlo_ready", b, j - 1)
                    dve.tensor_scalar(xs[:, j % 2, :], x_t[:, j, :], mv[:, j, 0:1], rstd[:, j:j + 1],
                                      ALU.subtract, ALU.mult).then_inc(S("xs_ready"), 1)

                def turn_low(j):
                    filled(dve, b, "xl", j)
                    if j == 0:
                        filled(dve, b, "v", TPB - 1, row=-1)
                    dve.tensor_copy(xT[:, 1, :, j * P:(j + 1) * P],
                                    half(USE["xl", j][0])[:, 0:DM].rearrange("p (c n) -> p c n", c=DC),
                                    ).then_inc(S("xTl_ready"), 1)

                moments(0)
                moments(1)
                normalize(0)
                moments(2)
                normalize(1)
                turn_low(0)
                moments(3)
                normalize(2)
                turn_low(1)
                normalize(3)
                turn_low(2)
                turn_low(3)

                filled(dve, b, "rt", 0)
                dve.tensor_copy(lg[:, :, :], bank[USE["rt", 0][0]][:, 0:TPB * 32].rearrange(
                    "p (j n) -> p j n", j=TPB)[:, :, 0:E + 1]).then_inc(S("logits_ready"), 1)
                wait(dve, "logits_ready", b, 1)
                dve.tensor_reduce(mx[:, :, :], lg[:, :, 0:E], AXX, ALU.max).then_inc(S("max_ready"), 1)
                wait(dve, "max_ready", b, 1)
                dve.tensor_tensor(delta[:, :, 0:E], lg[:, :, 0:E], mx[:, :, :].broadcast_to([P, TPB, E]),
                                  ALU.subtract).then_inc(S("delta_ready"), 1)
                dve.tensor_scalar(delta[:, :, E:E + 1], lg[:, :, E:E + 1], -1.0, None,
                                  ALU.mult).then_inc(S("delta_ready"), 1)

                def rotate(u):
                    wait(dve, "qs_ready", b, u + 1)
                    apart(dve)
                    dve.stream_shuffle(qswap[:, :], qs[:, u % 2, :], SWAP).then_inc(S("swap_done"), 1)
                    wait(dve, "swap_done", b, u + 1)
                    wait(dve, "qk_ready", b, u)
                    dve.tensor_tensor(qsin[:, :], qswap[:, :], T("sin"), ALU.mult).then_inc(S("sin_done"), 1)
                    wait(dve, "sin_done", b, u + 1)
                    wait(dve, "cos_done", b, u + 1)
                    if u == 0:
                        filled(dve, b, "inter", TPB - 1, row=-1)
                        filled(dve, b, "sc", TPB - 1, HQ - 1, row=-1)
                    dve.tensor_tensor(qkT[:, u, :], qcos[:, u % 2, :], qsin[:, :],
                                      ALU.add).then_inc(S("qk_ready"), 1)

                rotate(0)
                rotate(1)

                steps = [0]

                def step(ins):
                    ins.then_inc(S("route"), 1)
                    steps[0] += 1

                def settle():
                    wait(dve, "route", b, steps[0])

                wait(dve, "exp_ready", b, 2)
                apart(dve)
                for j in range(TPB):
                    step(dve.max(m8[:, j, :], pp[:, j, 0:E]))
                step(dve.tensor_scalar(sgy[:, :, :], sgx[:, :, :], 1.0, None, ALU.add))
                settle()
                step(dve.tensor_copy(msel[:, :, 0:TOPK], m8[:, :, 0:TOPK]))
                step(dve.tensor_reduce(wsum[:, :, :], m8[:, :, 0:TOPK], AXX, ALU.add))
                step(dve.reciprocal(wtok[:, :, TOPK:TOPK + 1], sgy[:, :, :]))
                settle()
                apart(dve)
                for j in range(TPB):
                    step(dve.match_replace(marked[:, j, :], msel[:, j, :], pp[:, j, :], -2.0))
                step(dve.reciprocal(wrec[:, :, :], wsum[:, :, :]))
                settle()
                filled(dve, b, "rank", 0, row=-1)
                dve.tensor_scalar(chosen[:, :, :], marked[:, :, 0:E], -1.5, None,
                                  ALU.is_lt).then_inc(S("chosen_ready"), 1)
                wait(dve, "chosen_ready", b, 1)
                step(dve.tensor_tensor(comb0[:, :, :], pp[:, :, 0:E], chosen[:, :, :], ALU.mult))
                settle()
                step(dve.tensor_tensor(comb[:, :, :], comb0[:, :, :], wrec[:, :, :].broadcast_to([P, TPB, E]),
                                       ALU.mult))
                for u in range(2, 2 * NG):
                    rotate(u)

                filled(dve, b, "rank", 0)
                ranks = bank[USE["rank", 0][0]][:, 0:2 * TPB * E].rearrange("p (a j n) -> p a j n", a=2, j=TPB)
                for j in range(TPB):
                    step(dve.tensor_tensor(count[:, j + 1, :], count[:, j, :], ranks[:, 1, j, :], ALU.add))
                    settle()
                dve.tensor_tensor(slot0[:, :, :], ranks[:, 0, :, :], count[:, 0:TPB, :],
                                  ALU.add).then_inc(S("rank_read"), 1)
                wait(dve, "rank_read", b, 1)
                for j in range(TPB):
                    step(dve.tensor_tensor(slot1[:, j, :], slot0[:, j, :], T("region"), ALU.add))
                step(dve.tensor_copy(count[:, 0, :], count[:, TPB, :]))
                settle()
                step(dve.tensor_tensor(key[:, :, :], slot1[:, :, :], chosen[:, :, :], ALU.mult))
                settle()
                apart(dve)
                for j in range(TPB):
                    step(dve.max(k8[:, j, :], key[:, j, :]))
                settle()
                wait(dve, "rows_sent", b, 0)
                dve.tensor_scalar(slots[:, :, :], k8[:, :, 0:TOPK], -1.0, None,
                                  ALU.add).then_inc(S("slots_ready"), 1)
                for j in range(TPB):
                    for k in range(TOPK):
                        step(dve.scalar_tensor_tensor(junk[:, j * TOPK + k, :], key[:, j, :], k8[:, j, k:k + 1],
                                                      comb[:, j, :], ALU.is_equal, ALU.mult,
                                                      accum_out=wtok[:, j, k:k + 1]))
                wait(dve, "slots_ready", b, 1)
                settle()
                step(dve.tensor_copy(slots_all[:, bass.ds(b * (TPB * TOPK), TPB * TOPK)],
                                     slots[:, :, :].rearrange("p j k -> p (j k)")))
                step(dve.tensor_copy(w_all[:, bass.ds(b * (TPB * (TOPK + 1)), TPB * (TOPK + 1))],
                                     wtok[:, :, :].rearrange("p j k -> p (j k)")))
                assert steps[0] == NROUTE, steps[0]

                def front(c):
                    if c < TPB - 1:
                        filled(dve, b, "kt", c)
                        filled(dve, b, "kv", (c - 1) % (TPB - 1), row=-1 if c == 0 else 0)
                        dve.tensor_tensor(kd[:, :], bank[USE["kt", c][0]][:, :], T("dk"),
                                          ALU.mult).then_inc(S("kd_ready"), 1)
                    for h in range(HQ):
                        filled(dve, b, "sc", c, h)
                        if h == 0:
                            filled(dve, b, "o", (c - 1) % TPB, row=-1 if c == 0 else 0)
                        dve.tensor_tensor(probs[:, h, :], bank[USE["sc", c, h][0]][:, :],
                                          T("mask")[:, h * NG * P:(h + 1) * NG * P],
                                          ALU.mult).then_inc(S("probs_ready"), 1)

                def middle(c):
                    filled(dve, b, "o", c)
                    if c:
                        filled(dve, b, "inter", c)
                        dve.tensor_tensor(inter[:, :], bank[USE["inter", c][0]][:, :], T("dq"),
                                          ALU.mult).then_inc(S("inter_done"), 1)
                        wait(dve, "inter_done", b, c)
                        dve.tensor_tensor(o_sum[:, :], bank[USE["o", c][0]][:, :], inter[:, :],
                                          ALU.add).then_inc(S("osum_done"), 1)
                    else:
                        dve.tensor_copy(o_sum[:, :], bank[USE["o", c][0]][:, :]).then_inc(S("osum_done"), 1)
                    wait(dve, "osum_done", b, c + 1)
                    wait(dve, "sig_ready", b, c + 1)
                    wait(dve, "sq_ready", b, c - 1)
                    dve.tensor_tensor(og[:, c % 2, :], o_sum[:, :], sig[:, c % 2, :],
                                      ALU.mult).then_inc(S("og_ready"), 1)
                    if c < TPB - 1:
                        filled(dve, b, "kv", c)
                        if c == 0:
                            filled(dve, b, "inter", TPB - 1, row=-1)
                            dve.tensor_tensor(state_in[:, :], bank[USE["kv", c][0]][:, :], T("bd"),
                                              ALU.mult).then_inc(S("kv_read"), 1)
                            wait(dve, "kv_read", b, 1)
                            dve.tensor_copy(state[:, :], state_in[:, :]).then_inc(S("state_ready"), 1)
                        else:
                            dve.tensor_tensor(state_in[:, :], bank[USE["kv", c][0]][:, :], T("bd"),
                                              ALU.mult).then_inc(S("kv_read"), 1)
                            dve.tensor_tensor(state[:, :], state[:, :], T("lam"),
                                              ALU.mult).then_inc(S("state_decayed"), 1)
                            wait(dve, "kv_read", b, c + 1)
                            wait(dve, "state_decayed", b, c)
                            dve.tensor_tensor(state[:, :], state[:, :], state_in[:, :],
                                              ALU.add).then_inc(S("state_ready"), 1)

                def sums(c):
                    wait(dve, "sq_ready", b, c + 1)
                    dve.tensor_reduce(ms[:, :], sq[:, :].rearrange("p (h d) -> p h d", h=NH), AXX,
                                      ALU.add).then_inc(S("ms_ready"), 1)

                def norm_o(c):
                    wait(dve, "rms_ready", b, c + 1)
                    wait(dve, "ohi_ready", b, c)
                    wait(dve, "olo_ready", b, c)
                    dve.tensor_tensor(on[:, :].rearrange("p (h d) -> p h d", h=NH),
                                      og[:, c % 2, :].rearrange("p (h d) -> p h d", h=NH),
                                      rms[:, :].rearrange("p (h o) -> p h o", o=1).broadcast_to([P, NH, HD]),
                                      ALU.mult).then_inc(S("on_ready"), 1)

                def turn_low_o(c):
                    filled(dve, b, "ol", c)
                    filled(dve, b, "wo", (c - 1) % TPB, row=-1 if c == 0 else 0)
                    dve.tensor_copy(oT[:, 1, :, :],
                                    half(USE["ol", c][0])[:, 0:DM].rearrange("p (c n) -> p c n", c=DC),
                                    ).then_inc(S("oTl_ready"), 1)

                for c in range(TPB):
                    front(c)
                    if c:
                        norm_o(c - 1)
                    middle(c)
                    sums(c)
                    if c:
                        turn_low_o(c - 1)
                norm_o(TPB - 1)
                turn_low_o(TPB - 1)

                wait(dve, "raw_in", b, LOOP["raw_in"][1])
                wait(dve, "am_ready", b, 0)
                for k in range(3):
                    dve.tensor_reduce(am_new[:, k:k + 1], stage[:, k, 0:2 * DM], AXX, ALU.max,
                                      apply_absolute_value=True).then_inc(S("raw_max"), 1)
                wait(dve, "raw_max", b, 3)
                dve.tensor_tensor(amax[:, 5:8], amax[:, 5:8], am_new[:, :],
                                  ALU.max).then_inc(S("am_ready"), 1)

            wait(dve, "route", NB - 1, NROUTE)
            dve.tensor_copy(count_i[:, :], count[:, TPB, :]).then_inc(counts_ready, 1)
            dve.wait_ge(counts_ready, 1)
            dve.wait_ge(emax_done, 1)
            barrier(dve, a_done)

            n_c = [0]

            def cstep(ins):
                ins.then_inc(cchain, 1)
                n_c[0] += 1
                dve.wait_ge(cchain, n_c[0])

            powers(5, 8, cchain, 0)
            n_c[0] = 4
            cstep(dve.tensor_scalar(inv_x[:, 5:8], inv_i[:, 5:8].bitcast(F32), 1 / XS, None, ALU.mult))
            cstep(dve.tensor_scalar(csc[:, 0:1], scale_of(5), 2.0 ** -33 / XS, None, ALU.mult))
            cstep(dve.tensor_tensor(csc[:, 2:3], inv_i[:, 5:6].bitcast(F32), inv_i[:, 6:7].bitcast(F32), ALU.mult))
            cstep(dve.tensor_scalar(csc[:, 3:4], csc[:, 2:3], 2.0 ** 33, None, ALU.mult))
            dve.tensor_tensor(csc[:, 1:2], csc[:, 3:4], inv_i[:, 7:8].bitcast(F32), ALU.mult).then_inc(csc_ready, 1)
            dve.wait_ge(csc_ready, 1)

            cstep(dve.tensor_scalar(count_i[:, :], count_i[:, :], P - 1.0, None, ALU.add))
            cstep(dve.tensor_scalar(tiles_i[:, :], count_i[:, :], 7, None, ALU.arith_shift_right))
            cstep(dve.tensor_copy(tcnt[:, :], tiles_i[:, :]))
            cstep(dve.tensor_copy(tsum[:, 0, :], tcnt[:, :]))
            for n in range(4):
                d = 1 << n
                cstep(dve.tensor_copy(tsum[:, n + 1, 0:d], tsum[:, n, 0:d]))
                cstep(dve.tensor_tensor(tsum[:, n + 1, d:E], tsum[:, n, d:E], tsum[:, n, 0:E - d], ALU.add))
            tiles = T("tiles")[0:1, :]
            cstep(dve.memset(expert_f[:, :], 0.0))
            cstep(dve.memset(before_f[:, :], 0.0))
            for e in range(E):
                end = tsum[0:1, 4, e:e + 1]
                cstep(dve.scalar_tensor_tensor(expert_f[:, :], tiles, end, expert_f[:, :], ALU.is_ge, ALU.add))
                cstep(dve.tensor_scalar(ge[:, :], tiles, end, tcnt[0:1, e:e + 1], ALU.is_ge, ALU.mult))
                cstep(dve.tensor_tensor(before_f[:, :], before_f[:, :], ge[:, :], ALU.add))
            cstep(dve.tensor_tensor(local_f[:, :], tiles, before_f[:, :], ALU.subtract))
            cstep(dve.tensor_scalar(rowbase_f[:, :], expert_f[:, :], float(REG), None, ALU.mult))
            dve.scalar_tensor_tensor(row_i[:, :], local_f[:, :], float(P), rowbase_f[:, :], ALU.mult,
                                     ALU.add).then_inc(meta_ready, 1)
            dve.tensor_scalar(off_i[:, :], expert_f[:, :], float(WEXP), None, ALU.mult).then_inc(meta_ready, 1)

            cstep(dve.tensor_scalar(shift[:, :], tcnt[:, :], float(P), -float(REG), ALU.mult, ALU.add))
            cstep(dve.tensor_copy(slots_f[:, :], slots_all[:, :]))
            cstep(dve.tensor_copy(ysum[:, :], slots_f[:, :]))
            for e in range(1, E):
                cstep(dve.tensor_scalar(moved[:, :], slots_f[:, :], float(e * REG), shift[:, e - 1:e], ALU.is_ge,
                                        ALU.mult))
                cstep(dve.tensor_tensor(ysum[:, :], ysum[:, :], moved[:, :], ALU.add))
            cstep(dve.tensor_copy(yrows[:, :], ysum[:, :]))
            cstep(dve.tensor_scalar(shared_row[:, :], tsum[0:1, 4, E - 1:E], float(P), None, ALU.mult))

            def split_low(e, i):
                dve.wait_ge(e_hi, e * 3 + 3)
                for k in range(3):
                    dve.scalar_tensor_tensor(expert_part(we, e, 1, k), raw_part(raw, i, k), scale_of(5 + k),
                                             expert_part(we, e, 0, k), ALU.mult, ALU.subtract).then_inc(e_lo, 1)

            with dve.Fori(0, E // 2) as e2:
                for i in range(2):
                    split_low(e2 * 2 + i, i)
            split_low(E, 0)

            def x_low(t, k):
                dve.wait_ge(turned, t + 1)
                dve.tensor_copy(xTc[:, k % 2, 1, :, :],
                                half(XL)[:, 0:DM].rearrange("p (c n) -> p c n", c=DC)).then_inc(xTc_lo, 1)

            def hidden(t, k, fresh):
                dve.wait_ge(sg_ready, t + 1)
                if not fresh:
                    dve.wait_ge(h_hi, t - 1)
                dve.scalar_tensor_tensor(hf[:, k % 2, :], bank[GUB + k % 2][:, FF:2 * FF], csc[:, 0:1],
                                         sg[:, k % 2, :], ALU.mult, ALU.mult).then_inc(h_ready, 1)
                dve.wait_ge(h_hi, t + 1)
                dve.tensor_tensor(h16[:, k % 2, 1, :], hf[:, k % 2, :], h16[:, k % 2, 0, :],
                                  ALU.subtract).then_inc(h_lo, 1)

            def h_read(t, k):
                dve.wait_ge(h_turned, t + 1)
                dve.tensor_copy(hT[:, k % 2, :, :],
                                half(HT)[:, 0:2 * P].rearrange("p (a n) -> p a n", a=2)).then_inc(hT_ready, 1)

            def tiles_of(base, first=False, last=False):
                for k in range(4):
                    t = base + k
                    if not (first and k == 0):
                        h_read(t - 1, (k - 1) % 4)
                    if not (last and k == 3):
                        x_low(t + 1, (k + 1) % 4)
                    hidden(t, k, first and k < 2)

            x_low(0, 0)
            tiles_of(0, first=True)
            with dve.Fori(1, NC4 - 1) as g:
                tiles_of(g * 4)
            tiles_of(CTILES - 4, last=True)
            h_read(CTILES - 1, 3)
            barrier(dve, c_done)

            def fetch(i, k):
                dve.tensor_copy(idx[:, k, :], yrows[:, bass.ds(i * TOPK, TOPK)]).then_inc(idx_ready, 1)

            def combine(i, k, last=False):
                n5 = TOPK + 1
                dve.wait_ge(gathered[k], i * 32 + (64 - 32 * k))
                dve.wait_ge(d_in[k], i * 24 + (48 - 24 * k))
                for n in range(n5):
                    wcol = w_all[:, bass.ds(i * n5 + n, 1)]
                    if n == 0:
                        ins = dve.tensor_scalar(acc[:, k, n, :], ygat[:, k, n, :], wcol, None, ALU.mult)
                    else:
                        src = ygat[:, k, n, :] if n < TOPK else ysh[:, k, :]
                        ins = dve.scalar_tensor_tensor(acc[:, k, n, :], src, wcol, acc[:, k, n - 1, :],
                                                       ALU.mult, ALU.add)
                    ins.then_inc(acc_done, 1)
                    dve.wait_ge(acc_done, i * n5 + (n + 1))
                if not last:
                    fetch(i + 2, k)

            def close(i, k, fresh):
                dve.wait_ge(silu_done, i + 1)
                dve.tensor_tensor(prod[:, k, :], gate_s[:, k, :], s_x[:, k, :], ALU.mult).then_inc(prod_done, 1)
                dve.wait_ge(prod_done, i + 1)
                if not fresh:
                    dve.wait_ge(res_out[k], i * 8 - 8 * k)
                dve.tensor_tensor(res[:, k, :], prod[:, k, :], x_d[:, k, :], ALU.add).then_inc(res_ready, 1)

            fetch(0, 0)
            fetch(1, 1)
            for k in range(2):
                combine(k, k)
                close(k, k, True)
            with dve.Fori(1, NT // 2 - 1) as g:
                for k in range(2):
                    combine(g * 2 + k, k)
                    close(g * 2 + k, k, False)
            for k in range(2):
                combine(NT - 2 + k, k, last=True)
                close(NT - 2 + k, k, False)

        @block.tensor
        def _(pe):
            credit(pe, [f"bank{i}_full" for i in range(8)])
            pe.wait_ge(tab_in, 64)
            pe.wait_ge(whi_ready, 5)
            pe.wait_ge(wlo_ready, 5)
            ident = T("ident")
            with pe.Fori(0, NB) as b:
                def dst(*stage):
                    return bank[USE[stage][0]]

                for j in range(TPB):
                    for s, lo, ready in (("xh", 0, "xhi_ready"), ("xl", DM, "xlo_ready")):
                        emptied(pe, b, s, j)
                        wait(pe, ready, b, j + 1)
                        for c in range(DC):
                            last = pe.transpose(half(USE[s, j][0])[:, c * P:(c + 1) * P],
                                                x16[:, j, lo + c * P:lo + (c + 1) * P], ident16)
                        last.then_inc(full((s, j)), 1)
                wait(pe, "xTh_ready", b, TPB)
                wait(pe, "xTl_ready", b, TPB)
                emptied(pe, b, "small", 0)
                sum_products(pe, dst("small", 0)[0:NSMALL, :], pair3(
                    lambda a_, c: ws16[:, a_, c, :], lambda a_, c: xT[:, a_, c, :], DC)).then_inc(full(("small", 0)), 1)
                for u in range(2 * NG):
                    if u == 1:
                        emptied(pe, b, "rt", 0)
                        wait(pe, "gT_ready", b, 1)
                        apart(pe)
                        for j in range(TPB):
                            last = pe.transpose(dst("rt", 0)[:, j * 32:j * 32 + E + 1],
                                                gT[0:E + 1, j * P:(j + 1) * P], ident[0:E + 1, 0:E + 1])
                        last.then_inc(full(("rt", 0)), 1)
                    w, g = w16["qk"[u // NG]], u % NG
                    emptied(pe, b, "qk", u)
                    sum_products(pe, dst("qk", u)[:, :], pair3(
                        lambda a_, c: w[:, a_, c, g * P:(g + 1) * P],
                        lambda a_, c: xT[:, a_, c, :], DC)).then_inc(full(("qk", u)), 1)
                for j in range(TPB):
                    emptied(pe, b, "v", j)
                    sum_products(pe, dst("v", j)[:, :], pair3(
                        lambda a_, c: xT[:, a_, c, j * P:(j + 1) * P],
                        lambda a_, c: w16["v"][:, a_, c, :], DC)).then_inc(full(("v", j)), 1)
                emptied(pe, b, "rank", 0)
                wait(pe, "chosen_ready", b, 1)
                for a_, m in enumerate((earlier, ones16)):
                    last = pe.matmul(dst("rank", 0)[:, a_ * TPB * E:(a_ + 1) * TPB * E], m,
                                     chosen[:, :, :].rearrange("p j n -> p (j n)"), start=True, stop=True)
                last.then_inc(full(("rank", 0)), 1)

                def front(c):
                    cols = slice(c * P, (c + 1) * P)
                    emptied(pe, b, "gate", c)
                    pe.matmul(dst("gate", c)[:, :], gT[HD:2 * HD, cols], wg2_sb[HD:2 * HD, :],
                              start=True, stop=True).then_inc(full(("gate", c)), 1)
                    if c == 0:
                        wait(pe, "qk_ready", b, 2 * NG)
                    if c < TPB - 1:
                        emptied(pe, b, "kt", c)
                        for g in range(NG):
                            last = pe.transpose(dst("kt", c)[:, g * P:(g + 1) * P], qkT[:, NG + g, cols], ident)
                        last.then_inc(full(("kt", c)), 1)
                    for h in range(HQ):
                        rows = slice(h * HD, (h + 1) * HD)
                        emptied(pe, b, "sc", c, h)
                        for g in range(NG):
                            last = pe.matmul(dst("sc", c, h)[:, g * P:(g + 1) * P], qkT[rows, NG + g, cols],
                                             qkT[rows, g, cols], start=True, stop=True)
                        last.then_inc(full(("sc", c, h)), 1)

                def middle(c):
                    cols = slice(c * P, (c + 1) * P)
                    emptied(pe, b, "o", c)
                    if c == 0:
                        wait(pe, "v_ready", b, TPB)
                    for h in range(HQ):
                        wait(pe, "probs_ready", b, c * HQ + h + 1)
                        for g in range(NG):
                            head = g * HQ + h
                            vc = slice(head * HD, (head + 1) * HD)
                            last = pe.matmul(dst("o", c)[:, vc], probs[:, h, g * P:(g + 1) * P],
                                             v_sb[:, c, vc], start=True, stop=True)
                    last.then_inc(full(("o", c)), 1)
                    if c:
                        emptied(pe, b, "inter", c)
                        wait(pe, "state_ready", b, c)
                        for g in range(NG):
                            last = pe.matmul(dst("inter", c)[:, g * P:(g + 1) * P], qkT[:, g, cols],
                                             state[:, g * P:(g + 1) * P], start=True, stop=True)
                        last.then_inc(full(("inter", c)), 1)
                    if c < TPB - 1:
                        emptied(pe, b, "kv", c)
                        wait(pe, "kd_ready", b, c + 1)
                        for g in range(NG):
                            last = pe.matmul(dst("kv", c)[:, g * P:(g + 1) * P], kd[:, g * P:(g + 1) * P],
                                             v_sb[:, c, g * P:(g + 1) * P], start=True, stop=True)
                        last.then_inc(full(("kv", c)), 1)

                def back(c):
                    for s, lo, ready in (("oh", 0, "ohi_ready"), ("ol", DM, "olo_ready")):
                        emptied(pe, b, s, c)
                        wait(pe, ready, b, c + 1)
                        for n in range(DC):
                            last = pe.transpose(half(USE[s, c][0])[:, n * P:(n + 1) * P],
                                                o16[:, lo + n * P:lo + (n + 1) * P], ident16)
                        last.then_inc(full((s, c)), 1)
                    wait(pe, "oTh_ready", b, c + 1)
                    wait(pe, "oTl_ready", b, c + 1)
                    emptied(pe, b, "wo", c)
                    sum_products(pe, dst("wo", c)[:, :], pair3(
                        lambda a_, n: oT[:, a_, n, :], lambda a_, n: w16["o"][:, a_, n, :],
                        DC)).then_inc(full(("wo", c)), 1)

                for c in range(TPB):
                    front(c)
                    middle(c)
                    if c:
                        back(c - 1)
                back(TPB - 1)
            barrier(pe, a_done)

            pe.wait_ge(meta_ready, 2)
            pe.wait_ge(e_hi, 3 * NE)
            pe.wait_ge(e_lo, 3 * NE)

            def weights_at(t):
                return pe.value_load(off_i[0:1, bass.ds(t, 1)], min_val=0, max_val=E * WEXP)

            def turn(t, k, fresh):
                if not fresh:
                    pe.wait_ge(xTc_hi, t)
                    pe.wait_ge(xTc_lo, t)
                pe.wait_ge(xin_ready[k], t * 4 + (16 - 4 * k))
                for i, dst in enumerate((half(XH), half(XL))):
                    for c in range(DC):
                        last = pe.transpose(dst[:, c * P:(c + 1) * P],
                                            xin[:, k, i * DM + c * P:i * DM + (c + 1) * P], ident16)
                last.then_inc(turned, 1)

            def gate_up(t, k, off, fresh):
                pe.wait_ge(xTc_hi, t + 1)
                pe.wait_ge(xTc_lo, t + 1)
                if not fresh:
                    pe.wait_ge(h_ready, t - 1)
                sum_products(pe, bank[GUB + k % 2][:, 0:GU], pair3(
                    lambda a_, c: xTc[:, k % 2, a_, c, :],
                    lambda a_, c: we[:, bass.ds(off + (a_ * DC + c) * GU, GU)], DC)).then_inc(gu_done, 1)

            def turn_h(t, k, fresh):
                pe.wait_ge(h_hi, t + 1)
                pe.wait_ge(h_lo, t + 1)
                if not fresh:
                    pe.wait_ge(hT_ready, t)
                for a_ in range(2):
                    last = pe.transpose(half(HT)[:, a_ * P:(a_ + 1) * P], h16[:, k % 2, a_, :], ident16)
                last.then_inc(h_turned, 1)

            def down(t, k, off, fresh):
                pe.wait_ge(hT_ready, t + 1)
                if not fresh:
                    pe.wait_ge(y_ready, t - 1)
                sum_products(pe, bank[YB + k % 2][:, :], pair3(
                    lambda a_, c: hT[:, k % 2, a_, :],
                    lambda a_, c: we[:, bass.ds(off + 2 * DC * GU + a_ * DM, DM)], 1)).then_inc(y_done, 1)

            def tiles_of(base, first=False, last=False):
                before = None if first else weights_at(base - 1)
                for k in range(4):
                    t = base + k
                    off = weights_at(t)
                    gate_up(t, k, off, first and k < 2)
                    if before is not None:
                        turn_h(t - 1, (k - 1) % 4, first and k == 1)
                    if not (last and k == 3):
                        turn(t + 1, (k + 1) % 4, False)
                    if before is not None:
                        down(t - 1, (k - 1) % 4, before, first and k < 3)
                    before = off
                return before

            turn(0, 0, True)
            tiles_of(0, first=True)
            with pe.Fori(1, NC4 - 1) as g:
                tiles_of(g * 4)
            off = tiles_of(CTILES - 4, last=True)
            turn_h(CTILES - 1, 3, False)
            down(CTILES - 1, 3, off, False)
            barrier(pe, c_done)


def expert_part(we, e, a_, k):
    if k == 2:
        return we[:, bass.ds(e * WEXP + 2 * DC * GU + a_ * DM, DM)]
    return we[:, bass.ds(e * WEXP + a_ * DC * GU, DC * GU)].rearrange(
        "p (c n) -> p c n", c=DC)[:, :, k * FF:(k + 1) * FF]


def raw_part(raw, i, k):
    if k == 2:
        return raw[:, i, k, :]
    return raw[:, i, k, :].rearrange("p (c n) -> p c n", c=DC)


_INS = ["x", "wq", "wk", "wv", "wo", "w_small", "wg2", "norm_w", "w_gate", "w_up", "w_down", "tab", "tab16"]


def kernel(L0_attn_x, L0_attn_Wq, L0_attn_Wk, L0_attn_Wv, L0_attn_Wo, L0_attn_Wg1, L0_attn_Wg2,
           L0_attn_norm_weight, L0_ffn_gate_w, L0_ffn_Wg, L0_ffn_Wu, L0_ffn_Wd, L0_ffn_sWg, L0_ffn_sWu,
           L0_ffn_sWd, L0_ffn_shared_gate_w):
    import concourse.bacc as _bacc
    from concourse.bass_utils import run_bass_kernel_spmd as _run

    small = np.zeros((DM, NSMALL), np.float32)
    small[:, 0:E] = np.asarray(L0_ffn_gate_w).T
    small[:, E:E + 1] = np.asarray(L0_ffn_shared_gate_w)
    small[:, HD:2 * HD] = np.asarray(L0_attn_Wg1)

    def with_shared(w, shared):
        return np.concatenate([np.asarray(w), np.asarray(shared)[None]], axis=0)

    tab, tab16 = tables()
    given = dict(
        x=np.asarray(L0_attn_x).reshape(NTOK, DM), wq=L0_attn_Wq, wk=L0_attn_Wk, wv=L0_attn_Wv, wo=L0_attn_Wo,
        w_small=small, wg2=L0_attn_Wg2, norm_w=L0_attn_norm_weight,
        w_gate=with_shared(L0_ffn_Wg, L0_ffn_sWg), w_up=with_shared(L0_ffn_Wu, L0_ffn_sWu),
        w_down=with_shared(L0_ffn_Wd, L0_ffn_sWd), tab=tab, tab16=tab16)
    nc = _bacc.Bacc("TRN2", target_bir_lowering=False, num_devices=1)
    arrays, args = {}, []
    for name in _INS:
        v = np.ascontiguousarray(given[name])
        arrays[f"in_{name}_dram"] = v
        args.append(nc.dram_tensor(f"in_{name}_dram", v.shape, mybir.dt.from_np(v.dtype), kind="ExternalInput").ap())
    args.append(nc.dram_tensor("out_0_dram", (NTOK, DM), F32, kind="ExternalOutput").ap())
    build(nc, *args)
    r = _run(nc, [arrays], core_ids=[0])
    return r.results[0]["out_0_dram"].reshape(NB, SEQ, DM)
```

```python
import concourse.bass as bass
from concourse import mybir
from contextlib import ExitStack
import numpy as np

F32 = mybir.dt.float32
F16 = mybir.dt.float16
I32 = mybir.dt.int32
ALU = mybir.AluOpType
ACT = mybir.ActivationFunctionType
AXX = mybir.AxisListType.X
ABSMAX = bass.bass_isa.ReduceOp.absmax

P = 128
NB, SEQ, DM = 8, 512, 512
NTOK = NB * SEQ
NT = NTOK // P
TPB = SEQ // P
DC = DM // P
NH, HD = 16, 32
HQ = P // HD
NG = NH // HQ
E, TOPK, FF = 16, 4, 128
NE = E + 1
REG = NTOK + P
CT = NTOK * TOPK // P + E
CTILES = CT + NT
ROWS = E * REG + NTOK + (CT - NTOK * TOPK // P) * P
WEXP = 2 * DC * 2 * FF + 2 * DM
GU = 2 * FF
XS = 256.0
LN_EPS, RMS_EPS = 1e-5, 1e-6
NKIND = 8
NROUTE = 47
NSMALL = 64
SWAP = [(i + HD // 2) % HD for i in range(HD)]

TAB = {}
_at = 0
for _name, _n in (("cos", SEQ), ("sin", SEQ), ("mask", NH * P), ("dk", DM), ("dq", DM), ("lam", NG * P),
                  ("bd", NG * P), ("ident", P), ("region", E), ("tiles", CTILES)):
    TAB[_name] = (_at, _n)
    _at += _n
NTAB = _at


def tables():
    f = np.float32
    t = np.zeros((P, NTAB), f)

    def put(name, a):
        at, n = TAB[name]
        t[:, at:at + n] = np.asarray(a, f).reshape(P, n)

    p = np.arange(P)
    theta = (10000.0 ** (-2.0 * np.arange(HD // 2) / HD)).astype(f)
    ang = np.arange(SEQ, dtype=f)[None, :] * theta[p % (HD // 2)][:, None]
    put("cos", np.cos(ang))
    put("sin", np.sin(ang) * np.where(p % HD < HD // 2, -1, 1)[:, None].astype(f))
    lam = -(2.0 ** (-8.0 * (np.arange(NH) + 1.0) / NH)).astype(f)
    head = np.arange(NG)[None, :] * HQ + np.arange(HQ)[:, None]
    diff = (p[None, :] - p[:, None]).astype(f)
    m = np.where(diff[:, None, None, :] >= 0,
                 np.exp(np.minimum(lam[head][None, :, :, None] * diff[:, None, None, :], 0)), 0)
    put("mask", m)
    lamd = np.repeat(lam, HD)[None, :]
    put("dk", np.exp(lamd * (P - 1.0 - p[:, None]).astype(f)))
    put("dq", np.exp(lam[head[p // HD]][:, :, None] * (p[None, None, :] + 1.0).astype(f)))
    same = (p[:, None] // HD == p[None, :] // HD).astype(f)
    put("bd", np.broadcast_to(same[:, None, :], (P, NG, P)))
    put("lam", np.exp(lam[head[p // HD]] * f(P))[:, :, None] * same[:, None, :])
    put("ident", np.eye(P))
    put("region", np.broadcast_to(np.arange(E) * REG + 1, (P, E)))
    put("tiles", np.broadcast_to(np.arange(CTILES), (P, CTILES)))
    h = np.zeros((P, 3 * P), np.float16)
    h[:, :P] = np.eye(P)
    h[:, P:2 * P] = p[:, None] < p[None, :]
    h[:, 2 * P:] = 1
    return t, h


def pass_a_order():
    order = [("qk", u) for u in range(2, 6)] + [("rank", 0)] + [("qk", u) for u in range(6, 2 * NG)]
    order += [("v", j) for j in range(TPB)] + [("gate", g) for g in range(NG)]
    for c in range(TPB):
        if c < TPB - 1:
            order += [("kt", c)]
        for h in range(HQ):
            order += [("sc", c, h)]
            if c == TPB - 1:
                order += [("xh", h), ("xl", h)]
        if c:
            order += [("ms", c - 1)]
        order += [("o", c)]
        if c < TPB - 1:
            order += [("kv", c)]
        if c:
            order += [("wo", c - 1)]
    return order + [("ms", TPB - 1), ("small", 0), ("qk", 0), ("rt", 0), ("qk", 1), ("wo", TPB - 1)]


def ahead(stage):
    return int(stage[0] in ("xh", "xl", "small", "rt") or stage[0] == "qk" and stage[1] < 2)


def pass_a_banks():
    use = {s: (i % 8, i // 8) for i, s in enumerate(pass_a_order())}
    per_turn = [sum(1 for b, _ in use.values() if b == i) for i in range(8)]
    return use, per_turn


def build(nc, x, wq, wk, wv, wo, w_small, wg2, norm_w, w_gate, w_up, w_down, tab_d, tab16_d, out):
    ctx = ExitStack()
    with ctx:
        def sb(name, shape, dt, where=ctx):
            return where.enter_context(nc.sbuf_tensor(name, shape, dt))

        def sem(name):
            return ctx.enter_context(nc.semaphore(name))

        xg = nc.dram_tensor("expert_rows", [ROWS, 2 * DM], F16, kind="Internal").ap()
        yg = nc.dram_tensor("expert_outputs", [CTILES * P, DM], F32, kind="Internal").ap()
        s_d = nc.dram_tensor("attention_out", [NTOK, DM], F32, kind="Internal").ap()

        bank = [ctx.enter_context(nc.psum_tensor(f"bank{i}", [P, 512], F32)) for i in range(8)]

        def half(i):
            return bank[i][:, :].bitcast(F16)

        tab = sb("tab", [P, NTAB], F32)
        tab16 = sb("tab16", [P, 3 * P], F16)
        ident16, earlier, ones16 = (tab16[:, i * P:(i + 1) * P] for i in range(3))

        def T(name):
            start, n = TAB[name]
            return tab[:, start:start + n]

        slots_all = sb("slots_all", [P, NT * TOPK], I32)
        w_all = sb("w_all", [P, NT * (TOPK + 1)], F32)
        yrows = sb("yrows", [P, NT * TOPK], I32)
        shared_row = sb("shared_row", [1, 1], I32)
        count = sb("count", [P, TPB + 1, E], F32)
        count_i = sb("count_i", [P, E], I32)
        amax = sb("amax", [P, NKIND], F32)
        amax_all = sb("amax_all", [P, NKIND], F32)
        bits = sb("bits", [P, NKIND], I32)
        sc_i = sb("sc_i", [P, NKIND], I32)
        inv_i = sb("inv_i", [P, NKIND], I32)
        inv_x = sb("inv_x", [P, NKIND], F32)
        am_new = sb("am_new", [P, 3], F32)
        neg_half = sb("neg_half", [P, 1], F32)
        rms_eps = sb("rms_eps", [P, 1], F32)

        def scale_of(k):
            return sc_i[:, k:k + 1].bitcast(F32)

        a = ExitStack()
        w16 = {n: sb(f"w16_{n}", [P, 2, DC, DM], F16, a) for n in "qkvo"}
        ws16 = sb("ws16", [P, 2, DC, NSMALL], F16, a)
        wg2_sb = sb("wg2_sb", [2 * HD, DM], F32, a)
        nw = sb("nw", [P, DC], F32, a)
        stage = sb("stage", [P, 4, DC * DM], F32, a)
        raw_small = sb("raw_small", [P, DC * NSMALL], F32, a)
        x_t = sb("x_t", [P, TPB, DM], F32, a)
        stats = sb("stats", [P, TPB, 6], F32, a)
        mv = sb("mv", [P, TPB, 2], F32, a)
        var_eps = sb("var_eps", [P, TPB], F32, a)
        rstd = sb("rstd", [P, TPB], F32, a)
        xs = sb("xs", [P, 2, DM], F32, a)
        x16 = sb("x16", [P, TPB, 2 * DM], F16, a)
        xT = sb("xT", [P, 2, DC, SEQ], F16, a)
        gT = sb("gT", [NSMALL, SEQ], F32, a)
        lg = sb("lg", [P, TPB, E + 1], F32, a)
        mx = sb("mx", [P, TPB, 1], F32, a)
        delta = sb("delta", [P, TPB, E + 1], F32, a)
        pp = sb("pp", [P, TPB, E + TOPK], F32, a)
        sgx = sb("sgx", [P, TPB, 1], F32, a)
        sgy = sb("sgy", [P, TPB, 1], F32, a)
        m8 = sb("m8", [P, TPB, 8], F32, a)
        msel = sb("msel", [P, TPB, 8], F32, a)
        marked = sb("marked", [P, TPB, E + TOPK], F32, a)
        chosen = sb("chosen", [P, TPB, E], F16, a)
        wsum = sb("wsum", [P, TPB, 1], F32, a)
        wrec = sb("wrec", [P, TPB, 1], F32, a)
        comb0 = sb("comb0", [P, TPB, E], F32, a)
        comb = sb("comb", [P, TPB, E], F32, a)
        slot0 = sb("slot0", [P, TPB, E], F32, a)
        slot1 = sb("slot1", [P, TPB, E], F32, a)
        key = sb("key", [P, TPB, E], F32, a)
        k8 = sb("k8", [P, TPB, 8], F32, a)
        slots = sb("slots", [P, TPB, TOPK], I32, a)
        wtok = sb("wtok", [P, TPB, TOPK + 1], F32, a)
        junk = sb("junk", [P, TPB * TOPK, E], F32, a)
        qs = sb("qs", [P, 2, SEQ], F32, a)
        qswap = sb("qswap", [P, SEQ], F32, a)
        qsin = sb("qsin", [P, SEQ], F32, a)
        qcos = sb("qcos", [P, 2, SEQ], F32, a)
        qkT = sb("qkT", [P, 2 * NG, SEQ], F32, a)
        raw_last = qkT[:, 0:3, :]
        v_sb = sb("v_sb", [P, TPB, DM], F32, a)
        sig = stage[:, 3, :].rearrange("p (g n) -> p g n", g=NG)
        kd = sb("kd", [P, DM], F32, a)
        probs = sb("probs", [P, HQ, NG * P], F32, a)
        state = sb("state", [P, NG * P], F32, a)
        state_in = sb("state_in", [P, NG * P], F32, a)
        qd = sb("qd", [P, DM], F32, a)
        og = sb("og", [P, DM], F32, a)
        sq = sb("sq", [P, DM], F32, a)
        std = sb("std", [P, DM], F32, a)
        on = sb("on", [P, DM], F32, a)
        oT = sb("oT", [P, 2, DC, P], F16, a)
        s_sb = sb("s_sb", [P, 2, DM], F32, a)
        zeros = sb("zeros", [P, 2 * DM], F16, a)
        a.close()

        c_ = ExitStack()
        we = sb("we", [P, NE * WEXP], F16, c_)
        raw = sb("raw", [P, 2, 3, DM], F32, c_)
        xin = sb("xin", [P, 4, 2 * DM], F16, c_)
        xTc = sb("xTc", [P, 2, 2, DC, P], F16, c_)
        sg = sb("sg", [P, 2, FF], F32, c_)
        hf = sb("hf", [P, 2, FF], F32, c_)
        h16 = sb("h16", [P, 2, 2, FF], F16, c_)
        hT = sb("hT", [P, 2, 2, P], F16, c_)
        y_sb = sb("y_sb", [P, 4, DM], F32, c_)
        tcnt = sb("tcnt", [P, E], F32, c_)
        tiles_i = sb("tiles_i", [P, E], I32, c_)
        tsum = sb("tsum", [P, 5, E], F32, c_)
        shift = sb("shift", [P, E], F32, c_)
        slots_f = sb("slots_f", [P, NT * TOPK], F32, c_)
        moved = sb("moved", [P, NT * TOPK], F32, c_)
        ysum = sb("ysum", [P, NT * TOPK], F32, c_)
        ge = sb("ge", [1, CTILES], F32, c_)
        expert_f = sb("expert_f", [1, CTILES], F32, c_)
        before_f = sb("before_f", [1, CTILES], F32, c_)
        local_f = sb("local_f", [1, CTILES], F32, c_)
        rowbase_f = sb("rowbase_f", [1, CTILES], F32, c_)
        row_i = sb("row_i", [1, CTILES], I32, c_)
        off_i = sb("off_i", [1, CTILES], I32, c_)
        csc = sb("csc", [P, 4], F32, c_)
        c_.close()

        d_ = ExitStack()
        ygat = sb("ygat", [P, 2, TOPK, DM], F32, d_)
        idx = sb("idx", [P, 2, TOPK], I32, d_)
        wd5 = sb("wd5", [P, 2, TOPK + 1], F32, d_)
        ysh = sb("ysh", [P, 2, DM], F32, d_)
        x_d = sb("x_d", [P, 2, DM], F32, d_)
        s_x = sb("s_x", [P, 2, DM], F32, d_)
        acc = sb("acc", [P, 2, TOPK + 1, DM], F32, d_)
        gate_s = sb("gate_s", [P, 2, DM], F32, d_)
        prod = sb("prod", [P, 2, DM], F32, d_)
        res = sb("res", [P, 2, DM], F32, d_)
        d_.close()

        LOOP = {}

        def lsem(name, n, rows=1):
            LOOP[name] = (sem(name), n, rows)

        USE, UPB = pass_a_banks()
        for i in range(8):
            lsem(f"bank{i}_full", UPB[i], 2)
        for j in range(TPB):
            lsem(f"x_in{j}", 16)
        for name, n in dict(
                stat_done=TPB, mv_ready=TPB, vareps_ready=TPB, rstd_ready=TPB, xs_ready=TPB,
                xhi_ready=TPB, xlo_ready=TPB, xTh_ready=TPB, xTl_ready=TPB, xrow_out=16 * TPB,
                gT_ready=1, logits_ready=1, max_ready=1, delta_ready=2, exp_ready=2, route=NROUTE,
                chosen_ready=1, rank_read=1, slots_ready=1, rows_sent=1,
                qs_ready=2 * NG, swap_done=2 * NG, sin_done=2 * NG, cos_done=2 * NG, qk_ready=2 * NG,
                v_ready=TPB, sig_ready=NG, kd_ready=TPB - 1, probs_ready=TPB * HQ, qd_ready=TPB - 1,
                og_ready=TPB, kv_read=TPB - 1, state_decayed=TPB - 2, state_ready=TPB - 1,
                sq_ready=TPB, std_ready=TPB, rec_done=TPB, on_ready=TPB, ohi_ready=TPB, olo_ready=TPB,
                s_ready=TPB, s_out0=8 * TPB, s_out1=8 * TPB,
                raw_in=16 * 5, raw_max=3, am_ready=1).items():
            lsem(name, n)

        def S(name):
            return LOOP[name][0]

        def at(name, r, m):
            _, n, rows = LOOP[name]
            return r[0] * n + ((r[1] + rows) * n + m)

        def wait(eng, name, r, m):
            value = at(name, r, m)
            if not (isinstance(value, int) and value <= 0):
                eng.wait_ge(S(name), value)

        def apart(eng):
            eng.nop(nofuse=True)

        def full(stage):
            return S(f"bank{USE[stage][0]}_full")

        def filled(eng, r, *stage, row=0):
            i, k = USE[stage]
            wait(eng, f"bank{i}_full", (r[0], r[1] + row - ahead(stage)), k + 1)

        READER = {}
        for j in range(TPB):
            READER["xh", j] = ("xTh_ready", j + 1)
            READER["xl", j] = ("xTl_ready", j + 1)
            READER["v", j] = ("v_ready", j + 1)
            READER["kt", j] = ("kd_ready", j + 1)
            READER["o", j] = ("og_ready", j + 1)
            READER["kv", j] = ("kv_read", j + 1)
            READER["ms", j] = ("std_ready", j + 1)
            READER["wo", j] = ("s_ready", j + 1)
            for h in range(HQ):
                READER["sc", j, h] = ("probs_ready", j * HQ + h + 1)
        for g in range(NG):
            READER["gate", g] = ("sig_ready", g + 1)
        for u in range(2 * NG):
            READER["qk", u] = ("qs_ready", u + 1)
        READER["small", 0] = ("gT_ready", 1)
        READER["rt", 0] = ("logits_ready", 1)
        READER["rank", 0] = ("rank_read", 1)
        BEFORE = {}
        for i in range(8):
            mine = sorted((s for s in USE if USE[s][0] == i), key=lambda s: USE[s][1])
            for n, s in enumerate(mine):
                BEFORE[s] = (mine[n - 1], -1 if n == 0 else 0)

        def emptied(eng, turn, *stage):
            before, row = BEFORE[stage]
            while isinstance(turn[0], int) and turn[0] == NB - 1 and row == 0 and ahead(before):
                before, row = BEFORE[before]
            name, m = READER[before]
            wait(eng, name, (turn[0], turn[1] + row + ahead(before)), m)

        scattered = sem("scattered")
        tab_in = sem("tab_in")
        tab16_in = sem("tab16_in")
        w_in = [sem(f"w_in_{n}") for n in "qkvo"]
        small_in = sem("small_in")
        last_in = sem("last_in")
        const_pool = sem("const_pool")
        const_dve = sem("const_dve")
        fold_done = sem("fold_done")
        amax_ready = sem("amax_ready")
        amax_done = sem("amax_done")
        scale_chain = sem("scale_chain")
        scale_ready = sem("scale_ready")
        whi_ready = sem("whi_ready")
        wlo_ready = sem("wlo_ready")
        zero_rows = sem("zero_rows")
        counts_ready = sem("counts_ready")
        a_done = sem("a_done")
        emax_done = sem("emax_done")
        cchain = sem("cchain")
        csc_ready = sem("csc_ready")
        meta_ready = sem("meta_ready")
        e_in = [sem(f"e_in{i}") for i in range(2)]
        e_hi = sem("e_hi")
        e_lo = sem("e_lo")
        xin_ready = [sem(f"xin_ready{i}") for i in range(4)]
        turned = sem("turned")
        xTc_hi = sem("xTc_hi")
        xTc_lo = sem("xTc_lo")
        gu_done = sem("gu_done")
        sg_ready = sem("sg_ready")
        h_ready = sem("h_ready")
        h_hi = sem("h_hi")
        h_lo = sem("h_lo")
        h_turned = sem("h_turned")
        hT_ready = sem("hT_ready")
        y_done = sem("y_done")
        y_ready = sem("y_ready")
        y_out = [sem(f"y_out{i}") for i in range(4)]
        c_done = sem("c_done")
        idx_ready = sem("idx_ready")
        gathered = [sem(f"gathered{i}") for i in range(2)]
        d_in = [sem(f"d_in{i}") for i in range(2)]
        acc_done = sem("acc_done")
        silu_done = sem("silu_done")
        prod_done = sem("prod_done")
        res_ready = sem("res_ready")
        res_out = [sem(f"res_out{i}") for i in range(2)]

        def contract_rows(w):
            return w.rearrange("(c p) n -> p c n", p=P)

        gate_v = w_gate.rearrange("e (c p) n -> e p c n", p=P)
        up_v = w_up.rearrange("e (c p) n -> e p c n", p=P)

        def credit(eng, names):
            for name in names:
                eng.sem_inc(S(name), LOOP[name][1])

        def barrier(eng, s):
            eng.drain().then_inc(s, 1)
            eng.wait_ge(s, 5)

        def pair3(lhs, rhs, n):
            return [(lhs(a_, c), rhs(b_, c)) for c in range(n) for a_, b_ in ((0, 0), (0, 1), (1, 0))]

        def sum_products(eng, dst, pairs):
            for n, (lhsT, rhs) in enumerate(pairs):
                last = eng.matmul(dst, lhsT, rhs, start=(n == 0), stop=(n == len(pairs) - 1))
            return last

        block = ctx.enter_context(nc.Block())
        NC4 = CTILES // 4
        XH, XL, HT, GUB, YB = 0, 1, 2, 3, 5

        @block.sync
        def _(sp):
            credit(sp, [f"x_in{j}" for j in range(TPB)] + ["xrow_out", "s_out0", "s_out1", "raw_in"])
            def load_x(r, j):
                wait(sp, "xs_ready", r, j + 1 - TPB)
                sp.dma_start(x_t[:, j, :], x[bass.ds(r[0] * SEQ + (r[1] * SEQ + j * P), P), :]).then_inc(
                    S(f"x_in{j}"), 16)

            def store_x(r, j):
                wait(sp, "xhi_ready", r, j + 1)
                wait(sp, "xlo_ready", r, j + 1)
                sp.dma_start(xg[bass.ds(r[0] * SEQ + (E * REG + r[1] * SEQ + j * P), P), :],
                             x16[:, j, :]).then_inc(S("xrow_out"), 16)

            FIRST = (-1, 1)
            sp.dma_start(tab16[:, :], tab16_d).then_inc(tab16_in, 16)
            for j in range(TPB):
                load_x(FIRST, j)
            sp.dma_start(nw[:, :], norm_w.rearrange("(c p) -> p c", p=P),
                         allow_slow_non_contiguous=True).then_inc(tab_in, 16)
            sp.dma_start(wg2_sb[HD:2 * HD, :], wg2).then_inc(tab_in, 16)
            for i, w in ((3, wo), (0, wq), (1, wk), (2, wv)):
                sp.dma_start(stage[:, i, :].rearrange("p (c n) -> p c n", c=DC),
                             contract_rows(w)).then_inc(w_in[i], 16)
            sp.dma_start(raw_small[:, :].rearrange("p (c n) -> p c n", c=DC),
                         contract_rows(w_small)).then_inc(small_in, 16)
            sp.dma_start(tab[:, :], tab_d).then_inc(tab_in, 16)
            for k, v in enumerate((gate_v[E], up_v[E])):
                sp.dma_start(raw_last[:, k, :].rearrange("p (c n) -> p c n", c=DC), v).then_inc(last_in, 16)
            sp.dma_start(raw_last[:, 2, :], w_down[E]).then_inc(last_in, 16)
            sp.wait_ge(const_pool, 3)
            for i in range((ROWS - E * REG - NTOK) // P):
                sp.dma_start(xg[E * REG + NTOK + i * P:E * REG + NTOK + (i + 1) * P, :],
                             zeros[:, :]).then_inc(zero_rows, 16)
            sp.wait_ge(wlo_ready, 5)
            sp.wait_ge(whi_ready, 5)
            for j in range(TPB):
                store_x(FIRST, j)

            def turn_of_a(b, last=False):
                row, following = (b, 0), (b, 1)
                wait(sp, "raw_max", row, 0)
                for i in range(2):
                    for k, v in enumerate((gate_v, up_v)):
                        sp.dma_start(stage[:, k, i * DM:(i + 1) * DM].rearrange("p (o c n) -> p o c n", o=1, c=DC),
                                     v[bass.ds(b * 2 + i, 1)].rearrange("o p c n -> p o c n")).then_inc(S("raw_in"), 16)
                sp.dma_start(stage[:, 2, 0:2 * DM].rearrange("p (o n) -> p o n", o=2),
                             w_down[bass.ds(b * 2, 2)].rearrange("o p n -> p o n")).then_inc(S("raw_in"), 16)
                if not last:
                    for j in range(TPB):
                        load_x(following, j)
                for c in range(TPB):
                    if c == 2 and not last:
                        for j in range(TPB):
                            store_x(following, j)
                    wait(sp, "s_ready", row, c + 1)
                    sp.dma_start(s_d[bass.ds(b * SEQ + c * P, P), :],
                                 s_sb[:, c % 2, :]).then_inc(S(f"s_out{c % 2}"), 16)

            with sp.Fori(0, NB - 1) as b:
                turn_of_a(b)
            turn_of_a(NB - 1, last=True)
            sp.wait_ge(counts_ready, 1)
            for e in range(E):
                n = sp.value_load(count_i[0:1, e:e + 1], min_val=0, max_val=NTOK)
                sp.dma_start(xg[bass.ds(n + e * REG, P), :], zeros[:, :]).then_inc(zero_rows, 16)
            sp.wait_ge(zero_rows, 16 * (E + (ROWS - E * REG - NTOK) // P))
            wait(sp, "s_out0", (NB - 1, 0), 8 * TPB)
            wait(sp, "s_out1", (NB - 1, 0), 8 * TPB)
            wait(sp, "xrow_out", (NB - 1, 0), 16 * TPB)
            barrier(sp, a_done)

            def load_expert(e, i):
                for k, v in enumerate((gate_v, up_v)):
                    sp.dma_start(raw[:, i, k, :].rearrange("p (o c n) -> p o c n", o=1, c=DC),
                                 v[bass.ds(e, 1)].rearrange("o p c n -> p o c n")).then_inc(e_in[i], 16)
                sp.dma_start(raw[:, i, 2, :].rearrange("p (o n) -> p o n", o=1),
                             w_down[bass.ds(e, 1)].rearrange("o p n -> p o n")).then_inc(e_in[i], 16)

            load_expert(0, 0)
            load_expert(1, 1)
            with sp.Fori(1, E // 2) as e2:
                for i in range(2):
                    sp.wait_ge(e_hi, e2 * 6 + (3 * i - 3))
                    sp.wait_ge(e_lo, e2 * 6 + (3 * i - 3))
                    load_expert(e2 * 2 + i, i)
            sp.wait_ge(e_hi, 3 * (E - 1))
            sp.wait_ge(e_lo, 3 * (E - 1))
            load_expert(E, 0)

            for k in range(4):
                sp.sem_inc(y_out[k], 16)
            sp.wait_ge(meta_ready, 2)

            def load_rows(t, k, first=False):
                row = sp.value_load(row_i[0:1, bass.ds(t, 1)], min_val=0, max_val=ROWS - P)
                if not first:
                    sp.wait_ge(turned, t - 3)
                sp.dma_start(xin[:, k, :], xg[bass.ds(row, P), :]).then_inc(xin_ready[k], 16)

            def store_rows(t, k):
                sp.wait_ge(y_ready, t + 1)
                sp.dma_start(yg[bass.ds(t * P, P), :], y_sb[:, k, :]).then_inc(y_out[k], 16)

            for k in range(4):
                load_rows(k, k, first=True)
            with sp.Fori(0, NC4 - 1) as g:
                for k in range(4):
                    load_rows(g * 4 + (k + 4), k)
                    store_rows(g * 4 + k, k)
            for k in range(4):
                store_rows(CTILES - 4 + k, k)
            for k in range(4):
                sp.wait_ge(y_out[k], 16 * (NC4 + 1))
            barrier(sp, c_done)

            shared = sp.value_load(shared_row[0:1, 0:1], min_val=0, max_val=CT * P)

            def load_d(i, k):
                sp.dma_start(x_d[:, k, :], x[bass.ds(i * P, P), :]).then_inc(d_in[k], 16)
                sp.dma_start(s_x[:, k, :], s_d[bass.ds(i * P, P), :]).then_inc(d_in[k], 16)
                sp.dma_start(ysh[:, k, :], yg[bass.ds(shared + i * P, P), :]).then_inc(d_in[k], 16)

            def store_d(i, k):
                sp.wait_ge(res_ready, i + 1)
                sp.dma_start(out[bass.ds(i * P, P), :], res[:, k, :]).then_inc(res_out[k], 16)

            for k in range(2):
                load_d(k, k)
            with sp.Fori(0, NT // 2 - 1) as g:
                for k in range(2):
                    store_d(g * 2 + k, k)
                    load_d(g * 2 + (k + 2), k)
            for k in range(2):
                store_d(NT - 2 + k, k)
            for k in range(2):
                sp.wait_ge(res_out[k], 16 * NT // 2)

        @block.gpsimd
        def _(pool):
            credit(pool, ["vareps_ready", "rstd_ready", "xlo_ready", "cos_done", "rows_sent", "qd_ready"])
            pool.memset(neg_half[:, :], -0.5).then_inc(const_pool, 1)
            pool.memset(rms_eps[:, :], RMS_EPS / XS ** 2).then_inc(const_pool, 1)
            pool.memset(zeros[:, :], 0.0).then_inc(const_pool, 1)
            pool.wait_ge(const_pool, 3)

            def rsqrt_var(r, j):
                wait(pool, "mv_ready", r, j + 1)
                apart(pool)
                pool.tensor_scalar(var_eps[:, j:j + 1], mv[:, j, 1:2], LN_EPS, 1 / XS ** 2, ALU.add,
                                   ALU.mult).then_inc(S("vareps_ready"), 1)
                wait(pool, "vareps_ready", r, j + 1)
                pool.tensor_tensor(rstd[:, j:j + 1], var_eps[:, j:j + 1], neg_half[:, 0:1],
                                   ALU.pow).then_inc(S("rstd_ready"), 1)

            def low(r, j):
                wait(pool, "xs_ready", r, j + 1)
                wait(pool, "xhi_ready", r, j + 1)
                filled(pool, r, "xl", j, row=-1)
                if j == 0:
                    wait(pool, "rows_sent", r, 0)
                    wait(pool, "xrow_out", r, 0)
                pool.tensor_tensor(x16[:, j, DM:2 * DM], xs[:, j % 2, :], x16[:, j, 0:DM],
                                   ALU.subtract).then_inc(S("xlo_ready"), 1)

            def decay_q(r, c):
                if c == 1:
                    wait(pool, "qk_ready", r, NG)
                    filled(pool, r, "o", TPB - 1, row=-1)
                else:
                    filled(pool, r, "o", c - 1)
                pool.tensor_tensor(qd[:, :].rearrange("p (g n) -> p g n", g=NG), qkT[:, 0:NG, c * P:(c + 1) * P],
                                   T("dq").rearrange("p (g n) -> p g n", g=NG),
                                   ALU.mult).then_inc(S("qd_ready"), 1)

            rsqrt_var((-1, 1), 0)
            rsqrt_var((-1, 1), 1)
            low((-1, 1), 0)
            rsqrt_var((-1, 1), 2)
            low((-1, 1), 1)
            rsqrt_var((-1, 1), 3)
            low((-1, 1), 2)
            low((-1, 1), 3)
            pool.wait_ge(amax_ready, 5)
            pool.partition_all_reduce(amax_all[:, 0:5], amax[:, 0:5], P, ABSMAX).then_inc(amax_done, 1)
            pool.wait_ge(tab_in, 48)

            def turn_of_a(b, last=False):
                row, following = (b, 0), (b, 1)
                for u in range(2 * NG):
                    wait(pool, "qs_ready", row, u + 1)
                    wait(pool, "qk_ready", row, u - 1)
                    apart(pool)
                    pool.tensor_tensor(qcos[:, u % 2, :], qs[:, u % 2, :], T("cos"),
                                       ALU.mult).then_inc(S("cos_done"), 1)
                wait(pool, "slots_ready", row, 1)
                apart(pool)
                for c in range(TPB):
                    for k in range(TOPK):
                        pool.indirect_dma_start(
                            out=xg, out_offset=bass.IndirectOffsetOnAxis(ap=slots[:, c, k:k + 1], axis=0),
                            in_=x16[:, c, :], in_offset=None).then_inc(scattered, 16)
                decay_q(row, 1)
                if not last:
                    rsqrt_var(following, 0)
                    rsqrt_var(following, 1)
                pool.wait_ge(scattered, b * (16 * TPB * TOPK) + 16 * TPB * TOPK)
                pool.sem_inc(S("rows_sent"), 1)
                decay_q(row, 2)
                if not last:
                    rsqrt_var(following, 2)
                    rsqrt_var(following, 3)
                    low(following, 0)
                    low(following, 1)
                decay_q(row, 3)
                if not last:
                    low(following, 2)
                    low(following, 3)

            with pool.Fori(0, NB - 1) as b:
                turn_of_a(b)
            turn_of_a(NB - 1, last=True)
            wait(pool, "am_ready", (NB - 1, 0), 1)
            pool.partition_all_reduce(amax_all[:, 5:8], amax[:, 5:8], P, ABSMAX).then_inc(emax_done, 1)
            pool.wait_ge(emax_done, 1)
            barrier(pool, a_done)
            barrier(pool, c_done)

            def gather(i, k):
                pool.wait_ge(idx_ready, i + 1)
                apart(pool)
                for n in range(TOPK):
                    pool.indirect_dma_start(
                        out=ygat[:, k, n, :], out_offset=None, in_=yg,
                        in_offset=bass.IndirectOffsetOnAxis(ap=idx[:, k, n:n + 1], axis=0),
                    ).then_inc(gathered[k], 16)

            with pool.Fori(0, NT // 2) as g:
                for k in range(2):
                    gather(g * 2 + k, k)

        @block.scalar
        def _(act):
            credit(act, ["xhi_ready", "xTh_ready", "gT_ready", "exp_ready", "qs_ready", "v_ready",
                         "sig_ready", "sq_ready", "std_ready", "ohi_ready", "s_ready"])

            def ix(k):
                return inv_x[:, k:k + 1]

            def high(r, j):
                wait(act, "xs_ready", r, j + 1)
                if j == 0:
                    wait(act, "rows_sent", r, 0)
                    wait(act, "xrow_out", r, 0)
                act.activation(x16[:, j, 0:DM], xs[:, j % 2, :], ACT.Copy).then_inc(S("xhi_ready"), 1)

            def turn_high(r, j):
                filled(act, r, "xh", j)
                if j == 0:
                    filled(act, r, "v", TPB - 1, row=-1)
                act.activation(xT[:, 0, :, j * P:(j + 1) * P],
                               half(USE["xh", j][0])[:, 0:DM].rearrange("p (c n) -> p c n", c=DC),
                               ACT.Copy).then_inc(S("xTh_ready"), 1)

            def small_read(r):
                filled(act, r, "small", 0)
                filled(act, r, "gate", NG - 1, row=-1)
                act.activation(gT[:, :], bank[USE["small", 0][0]][0:NSMALL, :], ACT.Copy,
                               scale=inv_x[0:NSMALL, 4:5]).then_inc(S("gT_ready"), 1)

            def exponents(r):
                wait(act, "delta_ready", r, 2)
                act.activation(pp[:, :, 0:E], delta[:, :, 0:E], ACT.Exp).then_inc(S("exp_ready"), 1)
                act.activation(sgx[:, :, :], delta[:, :, E:E + 1], ACT.Exp).then_inc(S("exp_ready"), 1)

            def silu_qk(r, u):
                filled(act, r, "qk", u)
                wait(act, "swap_done", r, u - 1)
                wait(act, "cos_done", r, u - 1)
                act.activation(qs[:, u % 2, :], bank[USE["qk", u][0]][:, :], ACT.Silu,
                               scale=ix(u // NG)).then_inc(S("qs_ready"), 1)

            def values(r, j):
                filled(act, r, "v", j)
                if j == 0:
                    filled(act, r, "o", TPB - 1, row=-1)
                    filled(act, r, "kv", TPB - 2, row=-1)
                act.activation(v_sb[:, j, :], bank[USE["v", j][0]][:, :], ACT.Copy,
                               scale=ix(2)).then_inc(S("v_ready"), 1)

            def gates(r, g):
                filled(act, r, "gate", g)
                wait(act, "og_ready", r, 0)
                act.activation(sig[:, g, :], bank[USE["gate", g][0]][:, :],
                               ACT.Sigmoid).then_inc(S("sig_ready"), 1)

            def squares(r, c):
                wait(act, "og_ready", r, c + 1)
                if c:
                    filled(act, r, "ms", c - 1)
                else:
                    filled(act, r, "ms", TPB - 1, row=-1)
                act.activation(sq[:, :], og[:, :], ACT.Square).then_inc(S("sq_ready"), 1)

            def roots(r, c):
                filled(act, r, "ms", c)
                wait(act, "rec_done", r, c)
                act.activation(std[:, :], bank[USE["ms", c][0]][:, :], ACT.Sqrt, bias=rms_eps[:, 0:1],
                               scale=1 / (HD * XS ** 2)).then_inc(S("std_ready"), 1)

            def high_o(r, c):
                wait(act, "on_ready", r, c + 1)
                if c:
                    filled(act, r, "wo", c - 1)
                else:
                    filled(act, r, "wo", TPB - 1, row=-1)
                act.activation(oT[:, 0, :, :].rearrange("p g n -> p (g n)"), on[:, :],
                               ACT.Copy).then_inc(S("ohi_ready"), 1)

            def finish(r, c):
                filled(act, r, "wo", c)
                wait(act, f"s_out{c % 2}", r, 16 * (c // 2))
                act.activation(s_sb[:, c % 2, :], bank[USE["wo", c][0]][:, :], ACT.Copy,
                               scale=ix(3)).then_inc(S("s_ready"), 1)

            high((-1, 1), 0)
            high((-1, 1), 1)
            turn_high((-1, 1), 0)
            high((-1, 1), 2)
            turn_high((-1, 1), 1)
            high((-1, 1), 3)
            turn_high((-1, 1), 2)
            turn_high((-1, 1), 3)
            act.wait_ge(scale_ready, 1)
            act.wait_ge(small_in, 16)
            act.activation(ws16[:, 0, :, :].rearrange("p c n -> p (c n)"), raw_small[:, :], ACT.Copy,
                           scale=scale_of(4)).then_inc(whi_ready, 1)
            for i, name in enumerate("qkvo"):
                act.activation(w16[name][:, 0, :, :].rearrange("p c n -> p (c n)"), stage[:, i, :], ACT.Copy,
                               scale=scale_of(i)).then_inc(whi_ready, 1)
            act.wait_ge(const_pool, 3)
            act.wait_ge(wlo_ready, 5)
            small_read((-1, 1))
            exponents((-1, 1))
            silu_qk((-1, 1), 0)
            silu_qk((-1, 1), 1)

            def turn_of_a(b, last=False):
                row, following = (b, 0), (b, 1)
                for u in range(2, 2 * NG):
                    silu_qk(row, u)
                for j in range(TPB):
                    values(row, j)
                for g in range(NG):
                    gates(row, g)
                squares(row, 0)
                for c in range(1, TPB):
                    if c == 3 and not last:
                        turn_high(following, 0)
                        high(following, 3)
                        for j in range(1, TPB):
                            turn_high(following, j)
                    roots(row, c - 1)
                    high_o(row, c - 1)
                    squares(row, c)
                    finish(row, c - 1)
                    if c == 1 and not last:
                        high(following, 0)
                        high(following, 1)
                    if c == 2 and not last:
                        high(following, 2)
                roots(row, TPB - 1)
                if not last:
                    small_read(following)
                high_o(row, TPB - 1)
                if not last:
                    exponents(following)
                    silu_qk(following, 0)
                    silu_qk(following, 1)
                finish(row, TPB - 1)

            with act.Fori(0, NB - 1) as b:
                turn_of_a(b)
            turn_of_a(NB - 1, last=True)
            barrier(act, a_done)

            act.wait_ge(csc_ready, 1)

            def split_high(e, i):
                act.wait_ge(e_in[i], e * 24 + (48 - 24 * i))
                for k in range(3):
                    act.activation(expert_part(we, e, 0, k), raw_part(raw, i, k), ACT.Copy,
                                   scale=scale_of(5 + k)).then_inc(e_hi, 1)

            with act.Fori(0, E // 2) as e2:
                for i in range(2):
                    split_high(e2 * 2 + i, i)
            split_high(E, 0)

            def x_high(t, k):
                act.wait_ge(turned, t + 1)
                act.activation(xTc[:, k % 2, 0, :, :],
                               half(XH)[:, 0:DM].rearrange("p (c n) -> p c n", c=DC),
                               ACT.Copy).then_inc(xTc_hi, 1)

            def silu_gate(t, k):
                act.wait_ge(gu_done, t + 1)
                act.activation(sg[:, k % 2, :], bank[GUB + k % 2][:, 0:FF], ACT.Silu,
                               scale=inv_x[:, 5:6]).then_inc(sg_ready, 1)

            def h_high(t, k):
                act.wait_ge(h_ready, t + 1)
                act.activation(h16[:, k % 2, 0, :], hf[:, k % 2, :], ACT.Copy).then_inc(h_hi, 1)

            def y_read(t, k):
                act.wait_ge(y_done, t + 1)
                act.wait_ge(y_out[k], t * 4 + (16 - 4 * k))
                act.activation(y_sb[:, k, :], bank[YB + k % 2][:, :], ACT.Copy,
                               scale=csc[:, 1:2]).then_inc(y_ready, 1)

            def tiles_of(base, first=False, last=False):
                for k in range(4):
                    t = base + k
                    silu_gate(t, k)
                    if not (last and k == 3):
                        x_high(t + 1, (k + 1) % 4)
                    if not (first and k == 0):
                        y_read(t - 1, (k - 1) % 4)
                    h_high(t, k)

            x_high(0, 0)
            tiles_of(0, first=True)
            with act.Fori(1, NC4 - 1) as g:
                tiles_of(g * 4)
            tiles_of(CTILES - 4, last=True)
            y_read(CTILES - 1, 3)
            barrier(act, c_done)

            def silu_d(i, k):
                act.wait_ge(acc_done, i * (TOPK + 1) + (TOPK + 1))
                act.activation(gate_s[:, k, :], acc[:, k, TOPK, :], ACT.Silu).then_inc(silu_done, 1)

            with act.Fori(0, NT // 2) as g:
                for k in range(2):
                    silu_d(g * 2 + k, k)

        @block.vector
        def _(dve):
            credit(dve, ["stat_done", "mv_ready", "xs_ready", "xTl_ready", "logits_ready", "max_ready",
                         "delta_ready", "route", "chosen_ready", "rank_read", "slots_ready", "swap_done",
                         "sin_done", "qk_ready", "kd_ready", "probs_ready", "og_ready", "rec_done", "kv_read",
                         "state_decayed", "state_ready", "on_ready", "olo_ready", "raw_max", "am_ready"])
            dve.memset(pp[:, :, E:E + TOPK], -1.0).then_inc(const_dve, 1)
            dve.memset(msel[:, :, TOPK:8], -1.0).then_inc(const_dve, 1)
            dve.memset(count[:, :, :], 0.0).then_inc(const_dve, 1)

            def moments(r, j):
                wait(dve, f"x_in{j}", r, 16)
                wait(dve, "mv_ready", r, j + 1 - TPB)
                dve.bn_stats(stats[:, j, :], x_t[:, j, :]).then_inc(S("stat_done"), 1)
                wait(dve, "stat_done", r, j + 1)
                wait(dve, "rstd_ready", r, j + 1 - TPB)
                apart(dve)
                dve.bn_aggr(mv[:, j, :], stats[:, j, :]).then_inc(S("mv_ready"), 1)

            def normalize(r, j):
                wait(dve, "rstd_ready", r, j + 1)
                wait(dve, "xhi_ready", r, j - 1)
                wait(dve, "xlo_ready", r, j - 1)
                dve.tensor_scalar(xs[:, j % 2, :], x_t[:, j, :], mv[:, j, 0:1], rstd[:, j:j + 1],
                                  ALU.subtract, ALU.mult).then_inc(S("xs_ready"), 1)

            def turn_low(r, j):
                filled(dve, r, "xl", j)
                if j == 0:
                    filled(dve, r, "v", TPB - 1, row=-1)
                dve.tensor_copy(xT[:, 1, :, j * P:(j + 1) * P],
                                half(USE["xl", j][0])[:, 0:DM].rearrange("p (c n) -> p c n", c=DC),
                                ).then_inc(S("xTl_ready"), 1)

            def logits(r):
                filled(dve, r, "rt", 0)
                wait(dve, "exp_ready", r, 0)
                dve.tensor_copy(lg[:, :, :], bank[USE["rt", 0][0]][:, 0:TPB * 32].rearrange(
                    "p (j n) -> p j n", j=TPB)[:, :, 0:E + 1]).then_inc(S("logits_ready"), 1)
                wait(dve, "logits_ready", r, 1)
                dve.tensor_reduce(mx[:, :, :], lg[:, :, 0:E], AXX, ALU.max).then_inc(S("max_ready"), 1)
                wait(dve, "max_ready", r, 1)
                dve.tensor_tensor(delta[:, :, 0:E], lg[:, :, 0:E], mx[:, :, :].broadcast_to([P, TPB, E]),
                                  ALU.subtract).then_inc(S("delta_ready"), 1)
                dve.tensor_scalar(delta[:, :, E:E + 1], lg[:, :, E:E + 1], -1.0, None,
                                  ALU.mult).then_inc(S("delta_ready"), 1)

            moments((-1, 1), 0)
            moments((-1, 1), 1)
            normalize((-1, 1), 0)
            moments((-1, 1), 2)
            normalize((-1, 1), 1)
            turn_low((-1, 1), 0)
            moments((-1, 1), 3)
            normalize((-1, 1), 2)
            turn_low((-1, 1), 1)
            normalize((-1, 1), 3)
            turn_low((-1, 1), 2)
            turn_low((-1, 1), 3)
            dve.wait_ge(tab_in, 48)
            dve.wait_ge(w_in[3], 16)
            for c in range(DC):
                dve.tensor_scalar(stage[:, 3, c * DM:(c + 1) * DM], stage[:, 3, c * DM:(c + 1) * DM],
                                  nw[:, c:c + 1], None, ALU.mult).then_inc(fold_done, 1)
            dve.wait_ge(fold_done, DC)
            dve.tensor_reduce(amax[:, 3:4], stage[:, 3, :], AXX, ALU.max,
                              apply_absolute_value=True).then_inc(amax_ready, 1)
            for i in range(3):
                dve.wait_ge(w_in[i], 16)
                dve.tensor_reduce(amax[:, i:i + 1], stage[:, i, :], AXX, ALU.max,
                                  apply_absolute_value=True).then_inc(amax_ready, 1)
            dve.wait_ge(small_in, 16)
            dve.tensor_reduce(amax[:, 4:5], raw_small[:, :], AXX, ALU.max,
                              apply_absolute_value=True).then_inc(amax_ready, 1)
            dve.wait_ge(last_in, 48)
            dve.tensor_reduce(amax[:, 5:8], raw_last[:, :, :], AXX, ALU.max,
                              apply_absolute_value=True).then_inc(amax_ready, 1)

            def powers(lo, hi, chain, n):
                k = slice(lo, hi)
                dve.tensor_scalar(amax_all[:, k], amax_all[:, k], 2.0 ** -60, None, ALU.max).then_inc(chain, 1)
                dve.wait_ge(chain, n + 1)
                dve.tensor_scalar(bits[:, k], amax_all[:, k].bitcast(I32), 0x7F800000, None,
                                  ALU.bitwise_and).then_inc(chain, 1)
                dve.wait_ge(chain, n + 2)
                dve.tensor_scalar(sc_i[:, k], bits[:, k], -1.0, float(268 << 23), ALU.mult,
                                  ALU.add).then_inc(chain, 1)
                dve.wait_ge(chain, n + 3)
                dve.tensor_scalar(inv_i[:, k], sc_i[:, k], -1.0, float(254 << 23), ALU.mult,
                                  ALU.add).then_inc(chain, 1)
                dve.wait_ge(chain, n + 4)

            dve.wait_ge(amax_done, 1)
            powers(0, 5, scale_chain, 0)
            dve.tensor_scalar(inv_x[:, 0:5], inv_i[:, 0:5].bitcast(F32), 1 / XS, None,
                              ALU.mult).then_inc(scale_ready, 1)
            dve.wait_ge(whi_ready, 1)
            dve.scalar_tensor_tensor(ws16[:, 1, :, :].rearrange("p c n -> p (c n)"), raw_small[:, :],
                                     scale_of(4), ws16[:, 0, :, :].rearrange("p c n -> p (c n)"),
                                     ALU.mult, ALU.subtract).then_inc(wlo_ready, 1)
            for i, name in enumerate("qkvo"):
                dve.wait_ge(whi_ready, i + 2)
                dve.scalar_tensor_tensor(w16[name][:, 1, :, :].rearrange("p c n -> p (c n)"), stage[:, i, :],
                                         scale_of(i), w16[name][:, 0, :, :].rearrange("p c n -> p (c n)"),
                                         ALU.mult, ALU.subtract).then_inc(wlo_ready, 1)
            dve.wait_ge(const_dve, 3)
            dve.wait_ge(amax_ready, 6)
            logits((-1, 1))

            def turn_of_a(b, last=False):
                row, following = (b, 0), (b, 1)

                def rotate(u):
                    wait(dve, "qs_ready", row, u + 1)
                    apart(dve)
                    dve.stream_shuffle(qswap[:, :], qs[:, u % 2, :], SWAP).then_inc(S("swap_done"), 1)
                    wait(dve, "swap_done", row, u + 1)
                    wait(dve, "qk_ready", row, u)
                    dve.tensor_tensor(qsin[:, :], qswap[:, :], T("sin"), ALU.mult).then_inc(S("sin_done"), 1)
                    wait(dve, "sin_done", row, u + 1)
                    wait(dve, "cos_done", row, u + 1)
                    if u == 0:
                        wait(dve, "qd_ready", row, 0)
                        filled(dve, row, "sc", TPB - 1, HQ - 1, row=-1)
                    dve.tensor_tensor(qkT[:, u, :], qcos[:, u % 2, :], qsin[:, :],
                                      ALU.add).then_inc(S("qk_ready"), 1)

                rotate(0)
                rotate(1)

                steps = [0]

                def step(ins):
                    ins.then_inc(S("route"), 1)
                    steps[0] += 1

                def settle():
                    wait(dve, "route", row, steps[0])

                wait(dve, "exp_ready", row, 2)
                apart(dve)
                for j in range(TPB):
                    step(dve.max(m8[:, j, :], pp[:, j, 0:E]))
                step(dve.tensor_scalar(sgy[:, :, :], sgx[:, :, :], 1.0, None, ALU.add))
                settle()
                step(dve.tensor_copy(msel[:, :, 0:TOPK], m8[:, :, 0:TOPK]))
                step(dve.tensor_reduce(wsum[:, :, :], m8[:, :, 0:TOPK], AXX, ALU.add))
                step(dve.reciprocal(wtok[:, :, TOPK:TOPK + 1], sgy[:, :, :]))
                settle()
                apart(dve)
                for j in range(TPB):
                    step(dve.match_replace(marked[:, j, :], msel[:, j, :], pp[:, j, :], -2.0))
                step(dve.reciprocal(wrec[:, :, :], wsum[:, :, :]))
                settle()
                filled(dve, row, "rank", 0, row=-1)
                dve.tensor_scalar(chosen[:, :, :], marked[:, :, 0:E], -1.5, None,
                                  ALU.is_lt).then_inc(S("chosen_ready"), 1)
                wait(dve, "chosen_ready", row, 1)
                step(dve.tensor_tensor(comb0[:, :, :], pp[:, :, 0:E], chosen[:, :, :], ALU.mult))
                settle()
                step(dve.tensor_tensor(comb[:, :, :], comb0[:, :, :], wrec[:, :, :].broadcast_to([P, TPB, E]),
                                       ALU.mult))
                for u in range(2, 2 * NG):
                    rotate(u)

                filled(dve, row, "rank", 0)
                ranks = bank[USE["rank", 0][0]][:, 0:2 * TPB * E].rearrange("p (a j n) -> p a j n", a=2, j=TPB)
                for j in range(TPB):
                    step(dve.tensor_tensor(count[:, j + 1, :], count[:, j, :], ranks[:, 1, j, :], ALU.add))
                    settle()
                dve.tensor_tensor(slot0[:, :, :], ranks[:, 0, :, :], count[:, 0:TPB, :],
                                  ALU.add).then_inc(S("rank_read"), 1)
                wait(dve, "rank_read", row, 1)
                for j in range(TPB):
                    step(dve.tensor_tensor(slot1[:, j, :], slot0[:, j, :], T("region"), ALU.add))
                step(dve.tensor_copy(count[:, 0, :], count[:, TPB, :]))
                settle()
                step(dve.tensor_tensor(key[:, :, :], slot1[:, :, :], chosen[:, :, :], ALU.mult))
                settle()
                apart(dve)
                for j in range(TPB):
                    step(dve.max(k8[:, j, :], key[:, j, :]))
                settle()
                wait(dve, "rows_sent", row, 0)
                dve.tensor_scalar(slots[:, :, :], k8[:, :, 0:TOPK], -1.0, None,
                                  ALU.add).then_inc(S("slots_ready"), 1)
                for j in range(TPB):
                    for k in range(TOPK):
                        step(dve.scalar_tensor_tensor(junk[:, j * TOPK + k, :], key[:, j, :], k8[:, j, k:k + 1],
                                                      comb[:, j, :], ALU.is_equal, ALU.mult,
                                                      accum_out=wtok[:, j, k:k + 1]))
                wait(dve, "slots_ready", row, 1)
                settle()
                step(dve.tensor_copy(slots_all[:, bass.ds(b * (TPB * TOPK), TPB * TOPK)],
                                     slots[:, :, :].rearrange("p j k -> p (j k)")))
                step(dve.tensor_copy(w_all[:, bass.ds(b * (TPB * (TOPK + 1)), TPB * (TOPK + 1))],
                                     wtok[:, :, :].rearrange("p j k -> p (j k)")))
                assert steps[0] == NROUTE, steps[0]

                def decayed_keys(c):
                    filled(dve, row, "kt", c)
                    filled(dve, row, "kv", (c - 1) % (TPB - 1), row=-1 if c == 0 else 0)
                    dve.tensor_tensor(kd[:, :], bank[USE["kt", c][0]][:, :], T("dk"),
                                      ALU.mult).then_inc(S("kd_ready"), 1)

                def masked(c, h):
                    filled(dve, row, "sc", c, h)
                    if h == 0:
                        filled(dve, row, "o", (c - 1) % TPB, row=-1 if c == 0 else 0)
                    dve.tensor_tensor(probs[:, h, :], bank[USE["sc", c, h][0]][:, :],
                                      T("mask")[:, h * NG * P:(h + 1) * NG * P],
                                      ALU.mult).then_inc(S("probs_ready"), 1)

                def gated(c):
                    filled(dve, row, "o", c)
                    if c == 0:
                        wait(dve, "sig_ready", row, NG)
                    wait(dve, "sq_ready", row, c)
                    wait(dve, "on_ready", row, c)
                    dve.tensor_tensor(og[:, :].rearrange("p (g n) -> p g n", g=NG),
                                      bank[USE["o", c][0]][:, :].rearrange("p (g n) -> p g n", g=NG),
                                      sig[:, :, c * P:(c + 1) * P], ALU.mult).then_inc(S("og_ready"), 1)

                def new_state(c):
                    filled(dve, row, "kv", c)
                    dve.tensor_tensor(state_in[:, :], bank[USE["kv", c][0]][:, :], T("bd"),
                                      ALU.mult).then_inc(S("kv_read"), 1)
                    if c == 0:
                        filled(dve, row, "o", TPB - 1, row=-1)
                        wait(dve, "kv_read", row, 1)
                        dve.tensor_copy(state[:, :], state_in[:, :]).then_inc(S("state_ready"), 1)
                    else:
                        dve.tensor_tensor(state[:, :], state[:, :], T("lam"),
                                          ALU.mult).then_inc(S("state_decayed"), 1)
                        wait(dve, "kv_read", row, c + 1)
                        wait(dve, "state_decayed", row, c)
                        dve.tensor_tensor(state[:, :], state[:, :], state_in[:, :],
                                          ALU.add).then_inc(S("state_ready"), 1)

                def normed(c):
                    wait(dve, "std_ready", row, c + 1)
                    apart(dve)
                    dve.reciprocal(on[:, :], std[:, :]).then_inc(S("rec_done"), 1)
                    wait(dve, "rec_done", row, c + 1)
                    wait(dve, "ohi_ready", row, c)
                    wait(dve, "olo_ready", row, c)
                    dve.tensor_tensor(on[:, :], og[:, :], on[:, :], ALU.mult).then_inc(S("on_ready"), 1)
                    wait(dve, "on_ready", row, c + 1)
                    wait(dve, "ohi_ready", row, c + 1)
                    apart(dve)
                    dve.tensor_tensor(oT[:, 1, :, :].rearrange("p g n -> p (g n)"), on[:, :],
                                      oT[:, 0, :, :].rearrange("p g n -> p (g n)"),
                                      ALU.subtract).then_inc(S("olo_ready"), 1)

                def magnitudes(k):
                    wait(dve, "raw_in", row, LOOP["raw_in"][1])
                    wait(dve, "am_ready", row, 0)
                    dve.tensor_reduce(am_new[:, k:k + 1], stage[:, k, 0:2 * DM], AXX, ALU.max,
                                      apply_absolute_value=True).then_inc(S("raw_max"), 1)

                for c in range(TPB):
                    if c < TPB - 1:
                        decayed_keys(c)
                    for h in range(HQ):
                        masked(c, h)
                        if c == TPB - 1 and not last:
                            if h == 0:
                                normalize(following, 3)
                            turn_low(following, h)
                    if c:
                        normed(c - 1)
                    gated(c)
                    if c < TPB - 1:
                        new_state(c)
                        magnitudes(c)
                    if last:
                        continue
                    if c == 0:
                        moments(following, 0)
                        moments(following, 1)
                    if c == 1:
                        moments(following, 2)
                        moments(following, 3)
                        normalize(following, 0)
                        normalize(following, 1)
                    if c == 2:
                        normalize(following, 2)
                wait(dve, "raw_max", row, 3)
                dve.tensor_tensor(amax[:, 5:8], amax[:, 5:8], am_new[:, :],
                                  ALU.max).then_inc(S("am_ready"), 1)
                normed(TPB - 1)
                if not last:
                    logits(following)

            with dve.Fori(0, NB - 1) as b:
                turn_of_a(b)
            turn_of_a(NB - 1, last=True)

            wait(dve, "route", (NB - 1, 0), NROUTE)
            dve.tensor_copy(count_i[:, :], count[:, TPB, :]).then_inc(counts_ready, 1)
            dve.wait_ge(counts_ready, 1)
            dve.wait_ge(emax_done, 1)
            barrier(dve, a_done)

            n_c = [0]

            def cstep(ins):
                ins.then_inc(cchain, 1)
                n_c[0] += 1
                dve.wait_ge(cchain, n_c[0])

            powers(5, 8, cchain, 0)
            n_c[0] = 4
            cstep(dve.tensor_scalar(inv_x[:, 5:8], inv_i[:, 5:8].bitcast(F32), 1 / XS, None, ALU.mult))
            cstep(dve.tensor_scalar(csc[:, 0:1], scale_of(5), 2.0 ** -33 / XS, None, ALU.mult))
            cstep(dve.tensor_tensor(csc[:, 2:3], inv_i[:, 5:6].bitcast(F32), inv_i[:, 6:7].bitcast(F32), ALU.mult))
            cstep(dve.tensor_scalar(csc[:, 3:4], csc[:, 2:3], 2.0 ** 33, None, ALU.mult))
            dve.tensor_tensor(csc[:, 1:2], csc[:, 3:4], inv_i[:, 7:8].bitcast(F32), ALU.mult).then_inc(csc_ready, 1)
            dve.wait_ge(csc_ready, 1)

            cstep(dve.tensor_scalar(count_i[:, :], count_i[:, :], P - 1.0, None, ALU.add))
            cstep(dve.tensor_scalar(tiles_i[:, :], count_i[:, :], 7, None, ALU.arith_shift_right))
            cstep(dve.tensor_copy(tcnt[:, :], tiles_i[:, :]))
            cstep(dve.tensor_copy(tsum[:, 0, :], tcnt[:, :]))
            for n in range(4):
                d = 1 << n
                cstep(dve.tensor_copy(tsum[:, n + 1, 0:d], tsum[:, n, 0:d]))
                cstep(dve.tensor_tensor(tsum[:, n + 1, d:E], tsum[:, n, d:E], tsum[:, n, 0:E - d], ALU.add))
            tiles = T("tiles")[0:1, :]
            cstep(dve.memset(expert_f[:, :], 0.0))
            cstep(dve.memset(before_f[:, :], 0.0))
            for e in range(E):
                end = tsum[0:1, 4, e:e + 1]
                cstep(dve.scalar_tensor_tensor(expert_f[:, :], tiles, end, expert_f[:, :], ALU.is_ge, ALU.add))
                cstep(dve.tensor_scalar(ge[:, :], tiles, end, tcnt[0:1, e:e + 1], ALU.is_ge, ALU.mult))
                cstep(dve.tensor_tensor(before_f[:, :], before_f[:, :], ge[:, :], ALU.add))
            cstep(dve.tensor_tensor(local_f[:, :], tiles, before_f[:, :], ALU.subtract))
            cstep(dve.tensor_scalar(rowbase_f[:, :], expert_f[:, :], float(REG), None, ALU.mult))
            dve.scalar_tensor_tensor(row_i[:, :], local_f[:, :], float(P), rowbase_f[:, :], ALU.mult,
                                     ALU.add).then_inc(meta_ready, 1)
            dve.tensor_scalar(off_i[:, :], expert_f[:, :], float(WEXP), None, ALU.mult).then_inc(meta_ready, 1)

            cstep(dve.tensor_scalar(shift[:, :], tcnt[:, :], float(P), -float(REG), ALU.mult, ALU.add))
            cstep(dve.tensor_copy(slots_f[:, :], slots_all[:, :]))
            cstep(dve.tensor_copy(ysum[:, :], slots_f[:, :]))
            for e in range(1, E):
                cstep(dve.tensor_scalar(moved[:, :], slots_f[:, :], float(e * REG), shift[:, e - 1:e], ALU.is_ge,
                                        ALU.mult))
                cstep(dve.tensor_tensor(ysum[:, :], ysum[:, :], moved[:, :], ALU.add))
            cstep(dve.tensor_copy(yrows[:, :], ysum[:, :]))
            cstep(dve.tensor_scalar(shared_row[:, :], tsum[0:1, 4, E - 1:E], float(P), None, ALU.mult))

            def split_low(e, i):
                dve.wait_ge(e_hi, e * 3 + 3)
                for k in range(3):
                    dve.scalar_tensor_tensor(expert_part(we, e, 1, k), raw_part(raw, i, k), scale_of(5 + k),
                                             expert_part(we, e, 0, k), ALU.mult, ALU.subtract).then_inc(e_lo, 1)

            with dve.Fori(0, E // 2) as e2:
                for i in range(2):
                    split_low(e2 * 2 + i, i)
            split_low(E, 0)

            def x_low(t, k):
                dve.wait_ge(turned, t + 1)
                dve.tensor_copy(xTc[:, k % 2, 1, :, :],
                                half(XL)[:, 0:DM].rearrange("p (c n) -> p c n", c=DC)).then_inc(xTc_lo, 1)

            def hidden(t, k, fresh):
                dve.wait_ge(sg_ready, t + 1)
                if not fresh:
                    dve.wait_ge(h_hi, t - 1)
                dve.scalar_tensor_tensor(hf[:, k % 2, :], bank[GUB + k % 2][:, FF:2 * FF], csc[:, 0:1],
                                         sg[:, k % 2, :], ALU.mult, ALU.mult).then_inc(h_ready, 1)
                dve.wait_ge(h_hi, t + 1)
                dve.tensor_tensor(h16[:, k % 2, 1, :], hf[:, k % 2, :], h16[:, k % 2, 0, :],
                                  ALU.subtract).then_inc(h_lo, 1)

            def h_read(t, k):
                dve.wait_ge(h_turned, t + 1)
                dve.tensor_copy(hT[:, k % 2, :, :],
                                half(HT)[:, 0:2 * P].rearrange("p (a n) -> p a n", a=2)).then_inc(hT_ready, 1)

            def tiles_of(base, first=False, last=False):
                for k in range(4):
                    t = base + k
                    if not (first and k == 0):
                        h_read(t - 1, (k - 1) % 4)
                    if not (last and k == 3):
                        x_low(t + 1, (k + 1) % 4)
                    hidden(t, k, first and k < 2)

            x_low(0, 0)
            tiles_of(0, first=True)
            with dve.Fori(1, NC4 - 1) as g:
                tiles_of(g * 4)
            tiles_of(CTILES - 4, last=True)
            h_read(CTILES - 1, 3)
            barrier(dve, c_done)

            def fetch(i, k):
                dve.tensor_copy(idx[:, k, :], yrows[:, bass.ds(i * TOPK, TOPK)]).then_inc(idx_ready, 1)

            def combine(i, k, last=False):
                n5 = TOPK + 1
                dve.wait_ge(gathered[k], i * 32 + (64 - 32 * k))
                dve.wait_ge(d_in[k], i * 24 + (48 - 24 * k))
                for n in range(n5):
                    wcol = w_all[:, bass.ds(i * n5 + n, 1)]
                    if n == 0:
                        ins = dve.tensor_scalar(acc[:, k, n, :], ygat[:, k, n, :], wcol, None, ALU.mult)
                    else:
                        src = ygat[:, k, n, :] if n < TOPK else ysh[:, k, :]
                        ins = dve.scalar_tensor_tensor(acc[:, k, n, :], src, wcol, acc[:, k, n - 1, :],
                                                       ALU.mult, ALU.add)
                    ins.then_inc(acc_done, 1)
                    dve.wait_ge(acc_done, i * n5 + (n + 1))
                if not last:
                    fetch(i + 2, k)

            def close(i, k, fresh):
                dve.wait_ge(silu_done, i + 1)
                dve.tensor_tensor(prod[:, k, :], gate_s[:, k, :], s_x[:, k, :], ALU.mult).then_inc(prod_done, 1)
                dve.wait_ge(prod_done, i + 1)
                if not fresh:
                    dve.wait_ge(res_out[k], i * 8 - 8 * k)
                dve.tensor_tensor(res[:, k, :], prod[:, k, :], x_d[:, k, :], ALU.add).then_inc(res_ready, 1)

            fetch(0, 0)
            fetch(1, 1)
            for k in range(2):
                combine(k, k)
                close(k, k, True)
            with dve.Fori(1, NT // 2 - 1) as g:
                for k in range(2):
                    combine(g * 2 + k, k)
                    close(g * 2 + k, k, False)
            for k in range(2):
                combine(NT - 2 + k, k, last=True)
                close(NT - 2 + k, k, False)

        @block.tensor
        def _(pe):
            credit(pe, [f"bank{i}_full" for i in range(8)])
            ident = T("ident")
            head_ones = T("bd")[:, 0:P]

            def dst(*stage):
                return bank[USE[stage][0]]

            ORDER = pass_a_order()

            def pass_over(turn, start, end):
                for i in range(8):
                    mine = [s for s in ORDER[start:end] if USE[s][0] == i]
                    if mine:
                        emptied(pe, turn, *mine[0])
                        apart(pe)
                        pe.sem_inc(S(f"bank{i}_full"), len(mine))

            def rows_to_columns(turn, j):
                for s, lo, ready in (("xh", 0, "xhi_ready"), ("xl", DM, "xlo_ready")):
                    emptied(pe, turn, s, j)
                    wait(pe, ready, (turn[0], turn[1] + 1), j + 1)
                    for c in range(DC):
                        last = pe.transpose(half(USE[s, j][0])[:, c * P:(c + 1) * P],
                                            x16[:, j, lo + c * P:lo + (c + 1) * P], ident16)
                    last.then_inc(full((s, j)), 1)

            def project_qk(turn, u):
                w, g = w16["qk"[u // NG]], u % NG
                emptied(pe, turn, "qk", u)
                sum_products(pe, dst("qk", u)[:, :], pair3(
                    lambda a_, c: w[:, a_, c, g * P:(g + 1) * P],
                    lambda a_, c: xT[:, a_, c, :], DC)).then_inc(full(("qk", u)), 1)

            def small_products(turn):
                emptied(pe, turn, "small", 0)
                apart(pe)
                wait(pe, "xTh_ready", (turn[0], turn[1] + 1), TPB)
                wait(pe, "xTl_ready", (turn[0], turn[1] + 1), TPB)
                sum_products(pe, dst("small", 0)[0:NSMALL, :], pair3(
                    lambda a_, c: ws16[:, a_, c, :], lambda a_, c: xT[:, a_, c, :], DC)).then_inc(full(("small", 0)), 1)
                project_qk(turn, 0)
                emptied(pe, turn, "rt", 0)
                wait(pe, "gT_ready", (turn[0], turn[1] + 1), 1)
                apart(pe)
                for j in range(TPB):
                    last = pe.transpose(dst("rt", 0)[:, j * 32:j * 32 + E + 1],
                                        gT[0:E + 1, j * P:(j + 1) * P], ident[0:E + 1, 0:E + 1])
                last.then_inc(full(("rt", 0)), 1)
                project_qk(turn, 1)

            before = (-1, 0)
            pass_over(before, 0, ORDER.index(("xh", 0)))
            pe.wait_ge(tab16_in, 16)
            for j in range(TPB):
                rows_to_columns(before, j)
                here = ORDER.index(("xl", j)) + 1
                pass_over(before, here, ORDER.index(("xh", j + 1)) if j < TPB - 1 else ORDER.index(("small", 0)))
            pe.wait_ge(tab_in, 48)
            pe.wait_ge(whi_ready, 5)
            pe.wait_ge(wlo_ready, 5)
            small_products(before)
            pass_over(before, ORDER.index(("qk", 1)) + 1, len(ORDER))

            def turn_of_a(b, last=False):
                row = (b, 0)
                for u in range(2, 6):
                    project_qk(row, u)
                emptied(pe, row, "rank", 0)
                wait(pe, "chosen_ready", row, 1)
                for a_, m in enumerate((earlier, ones16)):
                    ins = pe.matmul(dst("rank", 0)[:, a_ * TPB * E:(a_ + 1) * TPB * E], m,
                                    chosen[:, :, :].rearrange("p j n -> p (j n)"), start=True, stop=True)
                ins.then_inc(full(("rank", 0)), 1)
                for u in range(6, 2 * NG):
                    project_qk(row, u)
                for j in range(TPB):
                    emptied(pe, row, "v", j)
                    sum_products(pe, dst("v", j)[:, :], pair3(
                        lambda a_, c: xT[:, a_, c, j * P:(j + 1) * P],
                        lambda a_, c: w16["v"][:, a_, c, :], DC)).then_inc(full(("v", j)), 1)
                for g in range(NG):
                    emptied(pe, row, "gate", g)
                    pe.matmul(dst("gate", g)[:, :], wg2_sb[HD:2 * HD, g * P:(g + 1) * P], gT[HD:2 * HD, :],
                              start=True, stop=True).then_inc(full(("gate", g)), 1)

                def front(c):
                    cols = slice(c * P, (c + 1) * P)
                    if c < TPB - 1:
                        if c == 0:
                            wait(pe, "qk_ready", row, 2 * NG)
                        emptied(pe, row, "kt", c)
                        for g in range(NG):
                            ins = pe.transpose(dst("kt", c)[:, g * P:(g + 1) * P], qkT[:, NG + g, cols], ident)
                        ins.then_inc(full(("kt", c)), 1)
                    for h in range(HQ):
                        rows = slice(h * HD, (h + 1) * HD)
                        emptied(pe, row, "sc", c, h)
                        for g in range(NG):
                            ins = pe.matmul(dst("sc", c, h)[:, g * P:(g + 1) * P], qkT[rows, NG + g, cols],
                                            qkT[rows, g, cols], start=True, stop=True)
                        ins.then_inc(full(("sc", c, h)), 1)
                        if c == TPB - 1:
                            if last:
                                pass_over(row, ORDER.index(("xh", h)), ORDER.index(("xl", h)) + 1)
                            else:
                                rows_to_columns(row, h)

                def head_sums(c):
                    emptied(pe, row, "ms", c)
                    wait(pe, "sq_ready", row, c + 1)
                    pe.matmul(dst("ms", c)[:, :], head_ones, sq[:, :],
                              start=True, stop=True).then_inc(full(("ms", c)), 1)

                def middle(c):
                    emptied(pe, row, "o", c)
                    if c:
                        wait(pe, "state_ready", row, c)
                        wait(pe, "qd_ready", row, c)
                        for g in range(NG):
                            pe.matmul(dst("o", c)[:, g * P:(g + 1) * P], state[:, g * P:(g + 1) * P],
                                      qd[:, g * P:(g + 1) * P], start=(g == 0), stop=False)
                    else:
                        wait(pe, "v_ready", row, TPB)
                    for h in range(HQ):
                        wait(pe, "probs_ready", row, c * HQ + h + 1)
                        for g in range(NG):
                            head = g * HQ + h
                            ins = pe.matmul(dst("o", c)[h * HD:(h + 1) * HD, g * P:(g + 1) * P],
                                            v_sb[:, c, head * HD:(head + 1) * HD],
                                            probs[:, h, g * P:(g + 1) * P],
                                            start=(c == 0 and g == 0), stop=(g == NG - 1))
                    ins.then_inc(full(("o", c)), 1)
                    if c < TPB - 1:
                        emptied(pe, row, "kv", c)
                        wait(pe, "kd_ready", row, c + 1)
                        for g in range(NG):
                            ins = pe.matmul(dst("kv", c)[:, g * P:(g + 1) * P], kd[:, g * P:(g + 1) * P],
                                            v_sb[:, c, g * P:(g + 1) * P], start=True, stop=True)
                        ins.then_inc(full(("kv", c)), 1)

                def project_o(c):
                    wait(pe, "ohi_ready", row, c + 1)
                    wait(pe, "olo_ready", row, c + 1)
                    emptied(pe, row, "wo", c)
                    sum_products(pe, dst("wo", c)[:, :], pair3(
                        lambda a_, n: oT[:, a_, n, :], lambda a_, n: w16["o"][:, a_, n, :],
                        DC)).then_inc(full(("wo", c)), 1)

                for c in range(TPB):
                    front(c)
                    if c:
                        head_sums(c - 1)
                    middle(c)
                    if c:
                        project_o(c - 1)
                head_sums(TPB - 1)
                if last:
                    pass_over(row, ORDER.index(("small", 0)), ORDER.index(("qk", 1)) + 1)
                else:
                    small_products(row)
                project_o(TPB - 1)

            with pe.Fori(0, NB - 1) as b:
                turn_of_a(b)
            turn_of_a(NB - 1, last=True)
            barrier(pe, a_done)

            pe.wait_ge(meta_ready, 2)
            pe.wait_ge(e_hi, 3 * NE)
            pe.wait_ge(e_lo, 3 * NE)

            def weights_at(t):
                return pe.value_load(off_i[0:1, bass.ds(t, 1)], min_val=0, max_val=E * WEXP)

            def turn(t, k, fresh):
                if not fresh:
                    pe.wait_ge(xTc_hi, t)
                    pe.wait_ge(xTc_lo, t)
                pe.wait_ge(xin_ready[k], t * 4 + (16 - 4 * k))
                for i, dst in enumerate((half(XH), half(XL))):
                    for c in range(DC):
                        last = pe.transpose(dst[:, c * P:(c + 1) * P],
                                            xin[:, k, i * DM + c * P:i * DM + (c + 1) * P], ident16)
                last.then_inc(turned, 1)

            def gate_up(t, k, off, fresh):
                pe.wait_ge(xTc_hi, t + 1)
                pe.wait_ge(xTc_lo, t + 1)
                if not fresh:
                    pe.wait_ge(h_ready, t - 1)
                sum_products(pe, bank[GUB + k % 2][:, 0:GU], pair3(
                    lambda a_, c: xTc[:, k % 2, a_, c, :],
                    lambda a_, c: we[:, bass.ds(off + (a_ * DC + c) * GU, GU)], DC)).then_inc(gu_done, 1)

            def turn_h(t, k, fresh):
                pe.wait_ge(h_hi, t + 1)
                pe.wait_ge(h_lo, t + 1)
                if not fresh:
                    pe.wait_ge(hT_ready, t)
                for a_ in range(2):
                    last = pe.transpose(half(HT)[:, a_ * P:(a_ + 1) * P], h16[:, k % 2, a_, :], ident16)
                last.then_inc(h_turned, 1)

            def down(t, k, off, fresh):
                pe.wait_ge(hT_ready, t + 1)
                if not fresh:
                    pe.wait_ge(y_ready, t - 1)
                sum_products(pe, bank[YB + k % 2][:, :], pair3(
                    lambda a_, c: hT[:, k % 2, a_, :],
                    lambda a_, c: we[:, bass.ds(off + 2 * DC * GU + a_ * DM, DM)], 1)).then_inc(y_done, 1)

            def tiles_of(base, first=False, last=False):
                before = None if first else weights_at(base - 1)
                for k in range(4):
                    t = base + k
                    off = weights_at(t)
                    gate_up(t, k, off, first and k < 2)
                    if before is not None:
                        turn_h(t - 1, (k - 1) % 4, first and k == 1)
                    if not (last and k == 3):
                        turn(t + 1, (k + 1) % 4, False)
                    if before is not None:
                        down(t - 1, (k - 1) % 4, before, first and k < 3)
                    before = off
                return before

            turn(0, 0, True)
            tiles_of(0, first=True)
            with pe.Fori(1, NC4 - 1) as g:
                tiles_of(g * 4)
            off = tiles_of(CTILES - 4, last=True)
            turn_h(CTILES - 1, 3, False)
            down(CTILES - 1, 3, off, False)
            barrier(pe, c_done)


def expert_part(we, e, a_, k):
    if k == 2:
        return we[:, bass.ds(e * WEXP + 2 * DC * GU + a_ * DM, DM)]
    return we[:, bass.ds(e * WEXP + a_ * DC * GU, DC * GU)].rearrange(
        "p (c n) -> p c n", c=DC)[:, :, k * FF:(k + 1) * FF]


def raw_part(raw, i, k):
    if k == 2:
        return raw[:, i, k, :]
    return raw[:, i, k, :].rearrange("p (c n) -> p c n", c=DC)


_INS = ["x", "wq", "wk", "wv", "wo", "w_small", "wg2", "norm_w", "w_gate", "w_up", "w_down", "tab", "tab16"]


def kernel(L0_attn_x, L0_attn_Wq, L0_attn_Wk, L0_attn_Wv, L0_attn_Wo, L0_attn_Wg1, L0_attn_Wg2,
           L0_attn_norm_weight, L0_ffn_gate_w, L0_ffn_Wg, L0_ffn_Wu, L0_ffn_Wd, L0_ffn_sWg, L0_ffn_sWu,
           L0_ffn_sWd, L0_ffn_shared_gate_w):
    import concourse.bacc as _bacc
    from concourse.bass_utils import run_bass_kernel_spmd as _run

    small = np.zeros((DM, NSMALL), np.float32)
    small[:, 0:E] = np.asarray(L0_ffn_gate_w).T
    small[:, E:E + 1] = np.asarray(L0_ffn_shared_gate_w)
    small[:, HD:2 * HD] = np.asarray(L0_attn_Wg1)

    def with_shared(w, shared):
        return np.concatenate([np.asarray(w), np.asarray(shared)[None]], axis=0)

    tab, tab16 = tables()
    given = dict(
        x=np.asarray(L0_attn_x).reshape(NTOK, DM), wq=L0_attn_Wq, wk=L0_attn_Wk, wv=L0_attn_Wv, wo=L0_attn_Wo,
        w_small=small, wg2=L0_attn_Wg2, norm_w=L0_attn_norm_weight,
        w_gate=with_shared(L0_ffn_Wg, L0_ffn_sWg), w_up=with_shared(L0_ffn_Wu, L0_ffn_sWu),
        w_down=with_shared(L0_ffn_Wd, L0_ffn_sWd), tab=tab, tab16=tab16)
    nc = _bacc.Bacc("TRN2", target_bir_lowering=False, num_devices=1)
    arrays, args = {}, []
    for name in _INS:
        v = np.ascontiguousarray(given[name])
        arrays[f"in_{name}_dram"] = v
        args.append(nc.dram_tensor(f"in_{name}_dram", v.shape, mybir.dt.from_np(v.dtype), kind="ExternalInput").ap())
    args.append(nc.dram_tensor("out_0_dram", (NTOK, DM), F32, kind="ExternalOutput").ap())
    build(nc, *args)
    r = _run(nc, [arrays], core_ids=[0])
    return r.results[0]["out_0_dram"].reshape(NB, SEQ, DM)
```
